# Optimizing a Trainium2 kernel written in Bass

```python
import numpy as np
import jax
import jax.numpy as jnp

def _softmax(x, axis=-1):
    return jax.nn.softmax(x, axis=axis)

def _gelu(x):
    return jax.nn.gelu(x, approximate=True)

def _silu(x):
    return jax.nn.silu(x)

def _sigmoid(x):
    return jax.nn.sigmoid(x)

def _layernorm(x, axis=-1, eps=1e-05):
    m = jnp.mean(x, axis=axis, keepdims=True)
    v = jnp.var(x, axis=axis, keepdims=True)
    return (x - m) / jnp.sqrt(v + eps)

def _scatter_add(tgt, idx, src, axis=0):
    return tgt.at[idx].add(src)

def _segment_sum(src, seg, n):
    return jax.ops.segment_sum(src, seg, n)
kernel_name = 'mk_adj_preln_d2_adj_r2_2c888b'

def setup_inputs(seed: int=0):
    np.random.seed(seed)
    _w = jnp.asarray

    def _rec_inputs():
        import jax
        import jax.numpy as jnp
        _gk = jax.random.key(seed)
        x = -0.001003 + 1 * jax.random.normal(jax.random.fold_in(_gk, 1), (6144, 128), jnp.float32)
        _a = jax.random.bernoulli(jax.random.fold_in(_gk, 2), 0.000325521, (6144, 6144))
        adj = _a.astype(jnp.int32)
        return (x, adj)
    x, adj = _rec_inputs()

    def _L0_gnn_setup():
        import jax, jax.numpy as jnp
        import numpy as np
        M = 6144
        N = 6144
        D = 128
        TEMPERATURE = 0.07
        NEG_PAD = jnp.float32(-2 ** 32 + 1)
        key = jax.random.key(seed)
        k1, k2, k3, k4 = jax.random.split(key, 4)
        xx_anchor = jax.random.normal(k1, (M, D), dtype=jnp.float32)
        inp = jax.random.normal(k2, (N, D), dtype=jnp.float32)
        adj = (jax.random.uniform(k3, (M, N)) < 0.002).astype(jnp.int32)
        limit = jnp.sqrt(6.0 / (D + D)).astype(jnp.float32)
        weight = jax.random.uniform(k4, (D, D), minval=-limit, maxval=limit, dtype=jnp.float32)
        return {'xx_anchor': xx_anchor, 'input': inp, 'adj': adj, 'weight': weight}
    _L0_gnn_all = _L0_gnn_setup()
    _L0_gnn_in = {k: v for k, v in _L0_gnn_all.items() if k in ('input', 'weight')}
    del _L0_gnn_all

    def _L1_gnn_setup():
        import jax, jax.numpy as jnp
        import numpy as np
        N = 4096
        IN = 128
        OUT = 128
        THR = 0.0001
        ALPHA = 0.2
        NEG = -1000000000.0
        key = jax.random.key(seed)
        k1, k2, k3, k4 = jax.random.split(key, 4)
        inp = jax.random.normal(k1, (N, IN), jnp.float32)
        W = jax.random.normal(k2, (IN, OUT), jnp.float32) * (1.414 * np.sqrt(2.0 / (IN + OUT)))
        a = jax.random.normal(k3, (2 * OUT, 1), jnp.float32) * (1.414 * np.sqrt(2.0 / (2 * OUT + 1)))
        adj = jax.random.randint(k4, (N, N), 0, 2, jnp.int32)
        return {'input': inp, 'W': W, 'a': a, 'adj': adj, 'M': N}
    _L1_gnn_all = _L1_gnn_setup()
    _L1_gnn_in = {k: v for k, v in _L1_gnn_all.items() if k in ('W', 'a')}
    del _L1_gnn_all
    return {'x': x, 'adj': adj, 'L0_gnn_input': _L0_gnn_in['input'], 'L0_gnn_weight': _L0_gnn_in['weight'], 'L1_gnn_W': _L1_gnn_in['W'], 'L1_gnn_a': _L1_gnn_in['a']}

def reference(x, adj, L0_gnn_input, L0_gnn_weight, L1_gnn_W, L1_gnn_a):
    import jax
    import jax.numpy as jnp

    def _L0_gnn_ref(xx_anchor, input, adj, weight):
        import jax, jax.numpy as jnp
        import numpy as np
        M = 6144
        N = 6144
        D = 128
        TEMPERATURE = 0.07
        NEG_PAD = jnp.float32(-2 ** 32 + 1)
        anchor_adj = jnp.einsum('md,de,ne->mn', xx_anchor, weight, input)
        scores = jnp.where(adj > 0, anchor_adj, NEG_PAD)
        atten = jax.nn.softmax(scores / TEMPERATURE, axis=1)
        return atten @ input

    def _L1_gnn_ref(input, W, a, adj, M):
        import jax, jax.numpy as jnp
        import numpy as np
        N = 4096
        IN = 128
        OUT = 128
        THR = 0.0001
        ALPHA = 0.2
        NEG = -1000000000.0
        h = input @ W
        a_src = a[:OUT, 0]
        a_dst = a[OUT:, 0]
        e = jax.nn.leaky_relu((h[:M] @ a_src)[:, None] + (h @ a_dst)[None, :], negative_slope=ALPHA)
        valid = (adj[:M] > 0) & (h.sum(axis=1) != 0)[None, :]
        att = jax.nn.softmax(jnp.where(valid, e, NEG), axis=1)
        att = jnp.where(valid, att, 0.0)
        L = valid.sum(axis=1).astype(h.dtype)
        top = att.max(axis=1)
        attention = jnp.where(att >= THR, att, 0.0) * L[:, None]
        attention = jnp.where((top > THR)[:, None], attention, 0.0)
        h_prime = attention @ h
        return jax.nn.elu(h[:M] + h_prime)
    h = jnp.maximum(_layernorm(x, axis=-1), 0.0)
    x = x + _L0_gnn_ref(h, L0_gnn_input, adj, L0_gnn_weight)
    h = jnp.maximum(_layernorm(x, axis=-1), 0.0)
    x = x + _L1_gnn_ref(h, L1_gnn_W, L1_gnn_a, adj, 6144)
    return x

_drawn_inputs = setup_inputs


def setup_inputs(seed=0):
    import zlib

    import numpy as np

    out = dict(_drawn_inputs(seed))
    spreads = {}
    factors = {}
    for name, (base, spread) in spreads.items():
        noise = np.random.default_rng([zlib.crc32(name.encode()), seed]).standard_normal(out[name].shape)
        drawn = base * np.exp(spread * noise) if base else spread * noise
        out[name] = jnp.asarray(drawn.astype(out[name].dtype))
    for name, factor in factors.items():
        out[name] = (out[name] * factor).astype(out[name].dtype)
    return out
```

```python
import concourse.bass as bass
from concourse import mybir
from contextlib import ExitStack

F32 = mybir.dt.float32
I32 = mybir.dt.int32
U8 = mybir.dt.uint8
ALU = mybir.AluOpType
ACT = mybir.ActivationFunctionType
AX = mybir.AxisListType.X

P = 128
EPS = 1e-5
TEMPERATURE = 0.07
NEG_PAD = float(-2 ** 32 + 1)
NEG = -1000000000.0
THR = 0.0001
ALPHA = 0.2
RSQRT_SEED = float(0x5F3759DF)


class Chain:

    def __init__(self, eng, sem):
        self.eng, self.sem, self.n = eng, sem, 0

    def __call__(self, ins):
        self.n += 1
        ins.then_inc(self.sem, 1)
        self.eng.wait_ge(self.sem, self.n)

    def step(self):
        self.n += 1
        self.eng.sem_inc(self.sem, 1)
        self.eng.wait_ge(self.sem, self.n)

    def reset(self):
        self.eng.sem_clear(self.sem)
        self.n = 0


def rsqrt(nc, link, y, var, tmp, half):
    link(nc.vector.tensor_scalar(half, var, 0.5, None, ALU.mult))
    link(nc.vector.tensor_scalar(y.bitcast(I32), var.bitcast(I32), -0.5, RSQRT_SEED, ALU.mult, ALU.add))
    for _ in range(4):
        link(nc.vector.tensor_tensor(tmp, y, y, ALU.mult))
        link(nc.vector.tensor_tensor(tmp, tmp, half, ALU.mult))
        link(nc.vector.tensor_scalar(tmp, tmp, -1.0, 1.5, ALU.mult, ALU.add))
        link(nc.vector.tensor_tensor(y, y, tmp, ALU.mult))


def dense_path(nc, x, adj, inp, w0, w1, a, out):
    N, D = x.shape
    T = N // P
    C = 512
    NC = N // C
    Q = C // P
    x_v = x.rearrange("(t p) d -> p t d", p=P)
    inp_v = inp.rearrange("(t p) d -> p t d", p=P)
    out_v = out.rearrange("(t p) d -> p t d", p=P)
    a_v = a.rearrange("(k d) o -> d (k o)", k=2)

    with ExitStack() as ctx:
        def sb(name, shape, dt=F32):
            return ctx.enter_context(nc.sbuf_tensor("d_" + name, shape, dt))

        def sem(name):
            return ctx.enter_context(nc.semaphore("d_" + name))

        x_all = sb("x_all", [P, T, D])
        key_in = sb("key_in", [P, D])
        values = sb("values", [P, T, D])
        keys_t = sb("keys_t", [P, N])
        col_valid = sb("col_valid", [P, N], U8)
        adj_sb = sb("adj", [P, N], I32)
        mask = sb("mask", [P, N], U8)
        scores = sb("scores", [P, N])
        w_sb = sb("w", [P, 2, D])
        a_sb = sb("a", [P, 2])
        a_dst_b = sb("a_dst_b", [P, P])
        ones = sb("ones", [P, P])
        ident = sb("ident", [P, P])
        zero_c = sb("zero_c", [P, 1])
        stats = sb("stats", [P, 6])
        mv = sb("mv", [P, 2])
        rstd = sb("rstd", [P, 1])
        nt1 = sb("nt1", [P, 1])
        nt2 = sb("nt2", [P, 1])
        shift = sb("shift", [P, 1])
        hid = sb("hid", [P, D])
        hid_t = sb("hid_t", [P, P])
        proj_t = sb("proj_t", [P, P])
        src_all = sb("src_all", [P, T])
        dst_c = sb("dst_c", [P, P])
        leak = sb("leak", [P, 2, C])
        row_max = sb("row_max", [P, 1])
        row_sum = sb("row_sum", [P, 1])
        recip = sb("recip", [P, 1])
        top = sb("top", [P, 1])
        n_valid = sb("n_valid", [P, 1])
        factor = sb("factor", [P, 1])
        z = sb("z", [P, D])
        zneg = sb("zneg", [P, D])
        p_t = sb("p_t", [P, 2, C])

        def pb(name):
            return ctx.enter_context(nc.psum_tensor("d_" + name, [P, C], F32))
        sc_ps = [pb("sc0"), pb("sc1")]
        tp_ps = [pb("tp0"), pb("tp1")]
        out_ps = pb("out_ps")
        sm_ps = pb("sm_ps")

        loaded, chain = sem("loaded"), sem("chain")
        ident_z, ident_r, ones_r = sem("ident_z"), sem("ident_r"), sem("ones_r")
        bcast_r = sem("bcast_r")

        with nc.Block() as block:
            @block.sync
            def _(sp):
                sp.dma_start(x_all[:], x_v).then_inc(loaded, 16)
                sp.dma_start(values[:], inp_v).then_inc(loaded, 16)
                sp.dma_start(w_sb[:, 0, :], w0).then_inc(loaded, 16)
                sp.dma_start(w_sb[:, 1, :], w1).then_inc(loaded, 16)
                sp.dma_start(a_sb[:], a_v, allow_slow_non_contiguous=True).then_inc(loaded, 16)
                sp.wait_ge(loaded, 80)

            @block.gpsimd
            def _(pool):
                pool.memset(ident[:], 0.0).then_inc(ident_z, 1)
                pool.memset(ones[:], 1.0).then_inc(ones_r, 1)
                pool.memset(zero_c[:], 0.0)
                pool.wait_ge(ident_z, 1)
                pool.affine_select(out=ident[:], in_=ident[:], compare_op=ALU.not_equal, fill=1.0, base=0,
                                   pattern=[[-1, P]], channel_multiplier=1).then_inc(ident_r, 1)

            @block.vector
            def _(dve):
                dve.wait_ge(loaded, 80)
                dve.wait_ge(ones_r, 1)
                nc.vector.tensor_scalar(a_dst_b[:], ones[:], a_sb[:, 1:2], None, ALU.mult).then_inc(bcast_r, 1)

        def layer_norm_relu(link, xt):
            link(nc.vector.bn_stats(stats[:], xt))
            link(nc.vector.bn_aggr(mv[:], stats[:]))
            link(nc.vector.tensor_scalar(mv[:, 1:2], mv[:, 1:2], EPS, None, ALU.add))
            rsqrt(nc, link, rstd[:], mv[:, 1:2], nt1[:], nt2[:])
            link(nc.vector.tensor_scalar(hid[:], xt, mv[:, 0:1], rstd[:], ALU.subtract, ALU.mult))
            return nc.vector.tensor_scalar(hid[:], hid[:], 0.0, None, ALU.max)

        with nc.Block() as block:
            key_loaded, key_turned, key_kept = sem("key_loaded"), sem("key_turned"), sem("key_kept")

            @block.sync
            def _(sp):
                sp.sem_inc(key_turned, 1)
                with sp.Fori(0, T) as t:
                    sp.wait_ge(key_turned, t + 1)
                    sp.dma_start(key_in[:], inp_v[:, t, :]).then_inc(key_loaded, 16)

            @block.tensor
            def _(pe):
                pe.wait_ge(ident_r, 1)
                pe.sem_inc(key_kept, 1)
                with pe.Fori(0, T) as t:
                    pe.wait_ge(key_loaded, t * 16 + 16)
                    pe.wait_ge(key_kept, t + 1)
                    nc.tensor.transpose(tp_ps[0][:, 0:P], key_in[:], ident[:]).then_inc(key_turned, 1)

            @block.scalar
            def _(act):
                with act.Fori(0, T) as t:
                    act.wait_ge(key_turned, t + 2)
                    nc.scalar.copy(keys_t[:, bass.ds(t * P, P)], tp_ps[0][:, 0:P]).then_inc(key_kept, 1)

        def attention(layer):
            def lsem(name):
                return sem(f"{name}{layer}")

            adj_loaded, adj_used = lsem("adj_loaded"), lsem("adj_used")
            hid_r, hid_turned, hid_kept = lsem("hid_r"), lsem("hid_turned"), lsem("hid_kept")
            proj_r, proj_kept = lsem("proj_r"), lsem("proj_kept")
            score_r, score_used = lsem("score_r"), lsem("score_used")
            filled, centred, exp_r, weights_r = lsem("filled"), lsem("centred"), lsem("exp_r"), lsem("weights_r")
            turned, turned_kept, mixed = lsem("turned"), lsem("turned_kept"), lsem("mixed")
            pool_step = lsem("pool_step")
            z_r, e_r, row_done = lsem("z_r"), lsem("e_r"), lsem("row_done")

            with nc.Block() as block:
                @block.sync
                def _(sp):
                    sp.sem_inc(adj_used, 1)
                    with sp.Fori(0, T) as t:
                        sp.wait_ge(adj_used, t + 1)
                        sp.dma_start(adj_sb[:], adj[bass.ds(t * P, P), :]).then_inc(adj_loaded, 16)

                @block.gpsimd
                def _(pool):
                    pool.sem_inc(mixed, 1)
                    with pool.Fori(0, T) as t:
                        pool.wait_ge(mixed, t + 1)
                        pool.sem_inc(pool_step, 1)
                        pool.wait_ge(pool_step, 1)
                        pool.memset(scores[:], NEG if layer else NEG_PAD).then_inc(filled, 1)
                        pool.sem_clear(pool_step)

                @block.vector
                def _(dve):
                    link = Chain(dve, chain)
                    with dve.Fori(0, T) as t:
                        xt = x_all[:, t, :]
                        if layer == 0:
                            layer_norm_relu(link, xt).then_inc(hid_r, 1)
                        dve.wait_ge(adj_loaded, t * 16 + 16)
                        if layer == 0:
                            link(nc.vector.tensor_scalar(mask[:], adj_sb[:], 0.0, None, ALU.is_gt))
                        else:
                            link(nc.vector.scalar_tensor_tensor(mask[:], adj_sb[:], 0.0, col_valid[:],
                                                                ALU.is_gt, ALU.mult, accum_out=n_valid[:]))
                        dve.sem_inc(adj_used, 1)
                        dve.wait_ge(filled, t + 1)
                        for c in range(NC):
                            cs = slice(c * C, (c + 1) * C)
                            if layer == 0:
                                dve.wait_ge(score_r, t * NC + (c + 1))
                                link.step()
                                s_new = sc_ps[c % 2][:]
                            else:
                                s_new = leak[:, c % 2, :]
                                link(nc.vector.tensor_scalar(s_new, keys_t[:, cs], src_now[:], None, ALU.add)
                                     if c else nc.vector.tensor_copy(src_now[:], src_all[:, bass.ds(t, 1)]))
                                if c == 0:
                                    link(nc.vector.tensor_scalar(s_new, keys_t[:, cs], src_now[:], None, ALU.add))
                                link(nc.vector.scalar_tensor_tensor(s_new, s_new, ALPHA, s_new, ALU.mult, ALU.max))
                            last = nc.vector.copy_predicated(scores[:, cs], mask[:, cs], s_new)
                            if layer == 0:
                                last.then_inc(score_used, 1)
                        if layer == 0:
                            dve.wait_ge(score_used, t * NC + NC)
                        else:
                            link(last)
                        link(nc.vector.reduce_max(row_max[:], scores[:], AX))
                        nc.vector.tensor_scalar(scores[:], scores[:], row_max[:], None,
                                                ALU.subtract).then_inc(centred, 1)
                        dve.wait_ge(exp_r, t + 1)
                        last = nc.vector.reciprocal(recip[:], row_sum[:])
                        link(last)
                        if layer:
                            link(nc.vector.tensor_scalar(scores[:], scores[:], recip[:], None, ALU.mult))
                            link(nc.vector.tensor_tensor(scores[:], scores[:], mask[:], ALU.mult))
                            link(nc.vector.reduce_max(top[:], scores[:], AX))
                            link(nc.vector.scalar_tensor_tensor(factor[:], top[:], THR, n_valid[:], ALU.is_gt, ALU.mult))
                            link(nc.vector.scalar_tensor_tensor(scores[:], scores[:], THR, scores[:],
                                                                ALU.is_ge, ALU.mult))
                            dve.sem_inc(weights_r, 1)
                        dve.wait_ge(mixed, t + 2)
                        if layer == 0:
                            link(nc.vector.scalar_tensor_tensor(xt, out_ps[:, 0:D], recip[:], xt, ALU.mult, ALU.add))
                        else:
                            link(nc.vector.scalar_tensor_tensor(z[:], out_ps[:, 0:D], factor[:], values[:, t, :],
                                                                ALU.mult, ALU.add))
                            nc.vector.tensor_scalar(zneg[:], z[:], 0.0, None, ALU.min).then_inc(z_r, 1)
                            link(nc.vector.tensor_scalar(z[:], z[:], 0.0, -1.0, ALU.max, ALU.add))
                            dve.wait_ge(e_r, t + 1)
                            link(nc.vector.tensor_tensor(z[:], z[:], zneg[:], ALU.add))
                            link(nc.vector.tensor_tensor(xt, xt, z[:], ALU.add))
                        dve.sem_inc(row_done, 1)
                        link.reset()

                @block.scalar
                def _(act):
                    with act.Fori(0, T) as t:
                        if layer == 0:
                            act.wait_ge(hid_turned, t + 1)
                            nc.scalar.copy(hid_t[:], sm_ps[:, 0:P]).then_inc(hid_kept, 1)
                            act.wait_ge(proj_r, t + 1)
                            nc.scalar.copy(proj_t[:], sm_ps[:, P:2 * P]).then_inc(proj_kept, 1)
                        act.wait_ge(centred, t + 1)
                        nc.scalar.activation(scores[:], scores[:], ACT.Exp, bias=zero_c[:],
                                             scale=1.0 if layer else 1.0 / TEMPERATURE,
                                             accum_out=row_sum[:]).then_inc(exp_r, 1)
                        for c in range(NC):
                            act.wait_ge(turned, t * NC + (c + 1))
                            nc.scalar.copy(p_t[:, c % 2, :], tp_ps[c % 2][:]).then_inc(turned_kept, 1)
                        if layer:
                            act.wait_ge(z_r, t + 1)
                            nc.scalar.activation(zneg[:], zneg[:], ACT.Exp, bias=zero_c[:], scale=1.0).then_inc(e_r, 1)

                @block.tensor
                def _(pe):
                    def mix(c):
                        for q in range(Q):
                            k = c * Q + q
                            last = nc.tensor.matmul(out_ps[:, 0:D], p_t[:, c % 2, q * P:(q + 1) * P], values[:, k, :],
                                                    start=(k == 0), stop=(k == T - 1))
                        return last

                    pe.sem_inc(row_done, 1)
                    with pe.Fori(0, T) as t:
                        if layer == 0:
                            pe.wait_ge(hid_r, t + 1)
                            nc.tensor.transpose(sm_ps[:, 0:P], hid[:], ident[:]).then_inc(hid_turned, 1)
                            pe.wait_ge(hid_kept, t + 1)
                            nc.tensor.matmul(sm_ps[:, P:2 * P], w_sb[:, 0, :], hid_t[:],
                                             start=True, stop=True).then_inc(proj_r, 1)
                            pe.wait_ge(proj_kept, t + 1)
                            for c in range(NC):
                                if c >= 2:
                                    pe.wait_ge(score_used, t * NC + (c - 1))
                                nc.tensor.matmul(sc_ps[c % 2][:], proj_t[:], keys_t[:, c * C:(c + 1) * C],
                                                 start=True, stop=True).then_inc(score_r, 1)
                            pe.wait_ge(exp_r, t + 1)
                        else:
                            pe.wait_ge(weights_r, t + 1)
                        pe.wait_ge(row_done, t + 1)
                        for c in range(NC):
                            if c >= 2:
                                pe.wait_ge(turned_kept, t * NC + (c - 1))
                            for q in range(Q):
                                k = c * Q + q
                                last = nc.tensor.transpose(tp_ps[c % 2][:, q * P:(q + 1) * P],
                                                           scores[:, k * P:(k + 1) * P], ident[:])
                            last.then_inc(turned, 1)
                            if c:
                                pe.wait_ge(turned_kept, t * NC + c)
                                mix(c - 1).then_inc(mixed_part, 1)
                        pe.wait_ge(turned_kept, t * NC + NC)
                        mix(NC - 1).then_inc(mixed, 1)

        mixed_part = sem("mixed_part")
        src_now = sb("src_now", [P, 1])
        attention(0)

        hid_r, hid_turned, hid_kept = sem("hid_r"), sem("hid_turned"), sem("hid_kept")
        both_r, both_kept, parts_r, parts_kept = sem("both_r"), sem("both_kept"), sem("parts_r"), sem("parts_kept")
        valid_kept = sem("valid_kept")
        with nc.Block() as block:
            @block.vector
            def _(dve):
                link = Chain(dve, chain)
                with dve.Fori(0, T) as t:
                    layer_norm_relu(link, x_all[:, t, :]).then_inc(hid_r, 1)
                    dve.wait_ge(parts_r, t + 1)
                    link(nc.vector.tensor_scalar(col_valid[:, bass.ds(t * P, P)], out_ps[:, 0:P], 0.0, None,
                                                 ALU.not_equal))
                    dve.sem_inc(valid_kept, 1)
                    link.reset()

            @block.tensor
            def _(pe):
                pe.wait_ge(bcast_r, 1)
                pe.sem_inc(valid_kept, 1)
                with pe.Fori(0, T) as t:
                    pe.wait_ge(hid_r, t + 1)
                    nc.tensor.transpose(tp_ps[0][:, 0:P], hid[:], ident[:]).then_inc(hid_turned, 1)
                    pe.wait_ge(hid_kept, t + 1)
                    nc.tensor.matmul(tp_ps[1][:, 0:P], hid_t[:], w_sb[:, 1, :], start=True, stop=True)
                    nc.tensor.matmul(tp_ps[1][:, P:2 * P], w_sb[:, 1, :], hid_t[:], start=True,
                                     stop=True).then_inc(both_r, 1)
                    pe.wait_ge(both_kept, 2 * t + 2)
                    pe.wait_ge(valid_kept, t + 1)
                    nc.tensor.matmul(sm_ps[:, 0:P], a_dst_b[:], proj_t[:], start=True, stop=True)
                    nc.tensor.matmul(out_ps[:, 0:P], ones[:], proj_t[:], start=True, stop=True)
                    nc.tensor.matmul(sm_ps[:, 2 * P:2 * P + 1], proj_t[:], a_sb[:, 0:1], start=True,
                                     stop=True).then_inc(parts_r, 1)

            @block.scalar
            def _(act):
                with act.Fori(0, T) as t:
                    act.wait_ge(hid_turned, t + 1)
                    nc.scalar.copy(hid_t[:], tp_ps[0][:, 0:P]).then_inc(hid_kept, 1)
                    act.wait_ge(both_r, t + 1)
                    nc.scalar.copy(values[:, t, :], tp_ps[1][:, 0:P]).then_inc(both_kept, 1)
                    nc.scalar.copy(proj_t[:], tp_ps[1][:, P:2 * P]).then_inc(both_kept, 1)
                    act.wait_ge(parts_r, t + 1)
                    nc.scalar.copy(keys_t[:, bass.ds(t * P, P)], sm_ps[:, 0:P]).then_inc(parts_kept, 1)
                    nc.scalar.copy(src_all[:, bass.ds(t, 1)], sm_ps[:, 2 * P:2 * P + 1]).then_inc(parts_kept, 1)
                    act.wait_ge(parts_kept, 2 * t + 2)

        attention(1)

        stored = sem("stored")
        with nc.Block() as block:
            @block.sync
            def _(sp):
                sp.dma_start(out_v, x_all[:]).then_inc(stored, 16)
                sp.wait_ge(stored, 16)


INPUTS = ["x", "adj", "L0_gnn_input", "L0_gnn_weight", "L1_gnn_W", "L1_gnn_a"]


def kernel(**inputs):
    import numpy as np
    import concourse.bacc as bacc
    from concourse.bass_utils import run_bass_kernel_spmd

    nc = bacc.Bacc("TRN2", target_bir_lowering=False, num_devices=1)
    arrays, args = {}, []
    for name in INPUTS:
        array = np.ascontiguousarray(inputs[name])
        arrays["in_" + name] = array
        args.append(nc.dram_tensor("in_" + name, array.shape, mybir.dt.from_np(array.dtype), kind="ExternalInput").ap())
    out = nc.dram_tensor("out_x", arrays["in_x"].shape, F32, kind="ExternalOutput").ap()
    dense_path(nc, *args, out)
    result = run_bass_kernel_spmd(nc, [arrays], core_ids=[0])
    return result.results[0]["out_x"]
```

```python
import concourse.bass as bass
from concourse import mybir
from contextlib import ExitStack

F32 = mybir.dt.float32
BF16 = mybir.dt.bfloat16
I32 = mybir.dt.int32
U32 = mybir.dt.uint32
U8 = mybir.dt.uint8
ALU = mybir.AluOpType
ACT = mybir.ActivationFunctionType
AX = mybir.AxisListType.X

P = 128
EPS = 1e-5
TEMPERATURE = 0.07
NEG_PAD = float(-2 ** 32 + 1)
NEG = -1000000000.0
THR = 0.0001
ALPHA = 0.2
RSQRT_SEED = float(0x5F3759DF)
LIMIT = 0


class Chain:

    def __init__(self, eng, sem):
        self.eng, self.sem, self.n = eng, sem, 0

    def __call__(self, ins):
        self.n += 1
        ins.then_inc(self.sem, 1)
        self.eng.wait_ge(self.sem, self.n)

    def step(self):
        self.n += 1
        self.eng.sem_inc(self.sem, 1)
        self.eng.wait_ge(self.sem, self.n)

    def reset(self):
        self.eng.sem_clear(self.sem)
        self.n = 0


def rsqrt(nc, link, y, var, tmp, half):
    link(nc.vector.tensor_scalar(half, var, 0.5, None, ALU.mult))
    link(nc.vector.tensor_scalar(y.bitcast(I32), var.bitcast(I32), -0.5, RSQRT_SEED, ALU.mult, ALU.add))
    for _ in range(4):
        link(nc.vector.tensor_tensor(tmp, y, y, ALU.mult))
        link(nc.vector.tensor_tensor(tmp, tmp, half, ALU.mult))
        link(nc.vector.tensor_scalar(tmp, tmp, -1.0, 1.5, ALU.mult, ALU.add))
        link(nc.vector.tensor_tensor(y, y, tmp, ALU.mult))


def dense_path(nc, x, adj, inp, w0, w1, a, out):
    N, D = x.shape
    T = N // P
    C = 512
    NC = N // C
    Q = C // P
    x_v = x.rearrange("(t p) d -> p t d", p=P)
    inp_v = inp.rearrange("(t p) d -> p t d", p=P)
    out_v = out.rearrange("(t p) d -> p t d", p=P)
    a_v = a.rearrange("(k d) o -> d (k o)", k=2)

    with ExitStack() as ctx:
        def sb(name, shape, dt=F32):
            return ctx.enter_context(nc.sbuf_tensor("d_" + name, shape, dt))

        def sem(name):
            return ctx.enter_context(nc.semaphore("d_" + name))

        x_all = sb("x_all", [P, T, D])
        key_in = sb("key_in", [P, D])
        values = sb("values", [P, T, D])
        keys_t = sb("keys_t", [P, N])
        col_valid = sb("col_valid", [P, N], U8)
        adj_sb = sb("adj", [P, N], I32)
        mask = sb("mask", [P, N], U8)
        scores = sb("scores", [P, N])
        w_sb = sb("w", [P, 2, D])
        a_sb = sb("a", [P, 2])
        a_dst_b = sb("a_dst_b", [P, P])
        ones = sb("ones", [P, P])
        ident = sb("ident", [P, P])
        zero_c = sb("zero_c", [P, 1])
        stats = sb("stats", [P, 6])
        mv = sb("mv", [P, 2])
        rstd = sb("rstd", [P, 1])
        nt1 = sb("nt1", [P, 1])
        nt2 = sb("nt2", [P, 1])
        shift = sb("shift", [P, 1])
        hid = sb("hid", [P, D])
        hid_t = sb("hid_t", [P, P])
        proj_t = sb("proj_t", [P, P])
        src_all = sb("src_all", [P, T])
        dst_c = sb("dst_c", [P, P])
        leak = sb("leak", [P, 2, C])
        row_max = sb("row_max", [P, 1])
        row_sum = sb("row_sum", [P, 1])
        recip = sb("recip", [P, 1])
        top = sb("top", [P, 1])
        n_valid = sb("n_valid", [P, 1])
        factor = sb("factor", [P, 1])
        z = sb("z", [P, D])
        zneg = sb("zneg", [P, D])
        p_t = sb("p_t", [P, 2, C])

        def pb(name):
            return ctx.enter_context(nc.psum_tensor("d_" + name, [P, C], F32))
        sc_ps = [pb("sc0"), pb("sc1")]
        tp_ps = [pb("tp0"), pb("tp1")]
        out_ps = pb("out_ps")
        sm_ps = pb("sm_ps")

        loaded, chain = sem("loaded"), sem("chain")
        ident_z, ident_r, ones_r = sem("ident_z"), sem("ident_r"), sem("ones_r")
        bcast_r = sem("bcast_r")

        with nc.Block() as block:
            @block.sync
            def _(sp):
                sp.dma_start(x_all[:], x_v).then_inc(loaded, 16)
                sp.dma_start(values[:], inp_v).then_inc(loaded, 16)
                sp.dma_start(w_sb[:, 0, :], w0).then_inc(loaded, 16)
                sp.dma_start(w_sb[:, 1, :], w1).then_inc(loaded, 16)
                sp.dma_start(a_sb[:], a_v, allow_slow_non_contiguous=True).then_inc(loaded, 16)
                sp.wait_ge(loaded, 80)

            @block.gpsimd
            def _(pool):
                pool.memset(ident[:], 0.0).then_inc(ident_z, 1)
                pool.memset(ones[:], 1.0).then_inc(ones_r, 1)
                pool.memset(zero_c[:], 0.0)
                pool.wait_ge(ident_z, 1)
                pool.affine_select(out=ident[:], in_=ident[:], compare_op=ALU.not_equal, fill=1.0, base=0,
                                   pattern=[[-1, P]], channel_multiplier=1).then_inc(ident_r, 1)

            @block.vector
            def _(dve):
                dve.wait_ge(loaded, 80)
                dve.wait_ge(ones_r, 1)
                nc.vector.tensor_scalar(a_dst_b[:], ones[:], a_sb[:, 1:2], None, ALU.mult).then_inc(bcast_r, 1)

            @block.scalar
            def _(act):
                act.wait_ge(ident_r, 1)

            @block.tensor
            def _(pe):
                pe.wait_ge(ident_r, 1)

        def layer_norm_relu(link, xt):
            link(nc.vector.bn_stats(stats[:], xt))
            link(nc.vector.bn_aggr(mv[:], stats[:]))
            link(nc.vector.tensor_scalar(mv[:, 1:2], mv[:, 1:2], EPS, None, ALU.add))
            rsqrt(nc, link, rstd[:], mv[:, 1:2], nt1[:], nt2[:])
            link(nc.vector.tensor_scalar(hid[:], xt, mv[:, 0:1], rstd[:], ALU.subtract, ALU.mult))
            return nc.vector.tensor_scalar(hid[:], hid[:], 0.0, None, ALU.max)

        with nc.Block() as block:
            key_loaded, key_turned, key_kept = sem("key_loaded"), sem("key_turned"), sem("key_kept")

            @block.sync
            def _(sp):
                sp.sem_inc(key_turned, 1)
                with sp.Fori(0, T) as t:
                    sp.wait_ge(key_turned, t + 1)
                    sp.dma_start(key_in[:], inp_v[:, t, :]).then_inc(key_loaded, 16)

            @block.tensor
            def _(pe):
                pe.wait_ge(ident_r, 1)
                pe.sem_inc(key_kept, 1)
                with pe.Fori(0, T) as t:
                    pe.wait_ge(key_loaded, t * 16 + 16)
                    pe.wait_ge(key_kept, t + 1)
                    nc.tensor.transpose(tp_ps[0][:, 0:P], key_in[:], ident[:]).then_inc(key_turned, 1)

            @block.scalar
            def _(act):
                with act.Fori(0, T) as t:
                    act.wait_ge(key_turned, t + 2)
                    nc.scalar.copy(keys_t[:, bass.ds(t * P, P)], tp_ps[0][:, 0:P]).then_inc(key_kept, 1)

        def attention(layer):
            def lsem(name):
                return sem(f"{name}{layer}")

            adj_loaded, adj_used = lsem("adj_loaded"), lsem("adj_used")
            hid_r, hid_turned, hid_kept = lsem("hid_r"), lsem("hid_turned"), lsem("hid_kept")
            proj_r, proj_kept = lsem("proj_r"), lsem("proj_kept")
            score_r, score_used = lsem("score_r"), lsem("score_used")
            filled, centred, exp_r, weights_r = lsem("filled"), lsem("centred"), lsem("exp_r"), lsem("weights_r")
            turned, turned_kept, mixed = lsem("turned"), lsem("turned_kept"), lsem("mixed")
            pool_step = lsem("pool_step")
            z_r, e_r, row_done = lsem("z_r"), lsem("e_r"), lsem("row_done")

            with nc.Block() as block:
                @block.sync
                def _(sp):
                    sp.sem_inc(adj_used, 1)
                    with sp.Fori(0, T) as t:
                        sp.wait_ge(adj_used, t + 1)
                        sp.dma_start(adj_sb[:], adj[bass.ds(t * P, P), :]).then_inc(adj_loaded, 16)

                @block.gpsimd
                def _(pool):
                    pool.sem_inc(mixed, 1)
                    with pool.Fori(0, T) as t:
                        pool.wait_ge(mixed, t + 1)
                        pool.sem_inc(pool_step, 1)
                        pool.wait_ge(pool_step, 1)
                        pool.memset(scores[:], NEG if layer else NEG_PAD).then_inc(filled, 1)
                        pool.sem_clear(pool_step)

                @block.vector
                def _(dve):
                    link = Chain(dve, chain)
                    with dve.Fori(0, T) as t:
                        xt = x_all[:, t, :]
                        if layer == 0:
                            layer_norm_relu(link, xt).then_inc(hid_r, 1)
                        dve.wait_ge(adj_loaded, t * 16 + 16)
                        if layer == 0:
                            link(nc.vector.tensor_scalar(mask[:], adj_sb[:], 0.0, None, ALU.is_gt))
                        else:
                            link(nc.vector.scalar_tensor_tensor(mask[:], adj_sb[:], 0.0, col_valid[:],
                                                                ALU.is_gt, ALU.mult, accum_out=n_valid[:]))
                        dve.sem_inc(adj_used, 1)
                        dve.wait_ge(filled, t + 1)
                        for c in range(NC):
                            cs = slice(c * C, (c + 1) * C)
                            if layer == 0:
                                dve.wait_ge(score_r, t * NC + (c + 1))
                                link.step()
                                s_new = sc_ps[c % 2][:]
                            else:
                                s_new = leak[:, c % 2, :]
                                link(nc.vector.tensor_scalar(s_new, keys_t[:, cs], src_now[:], None, ALU.add)
                                     if c else nc.vector.tensor_copy(src_now[:], src_all[:, bass.ds(t, 1)]))
                                if c == 0:
                                    link(nc.vector.tensor_scalar(s_new, keys_t[:, cs], src_now[:], None, ALU.add))
                                link(nc.vector.scalar_tensor_tensor(s_new, s_new, ALPHA, s_new, ALU.mult, ALU.max))
                            last = nc.vector.copy_predicated(scores[:, cs], mask[:, cs], s_new)
                            if layer == 0:
                                last.then_inc(score_used, 1)
                        if layer == 0:
                            dve.wait_ge(score_used, t * NC + NC)
                        else:
                            link(last)
                        link(nc.vector.reduce_max(row_max[:], scores[:], AX))
                        nc.vector.tensor_scalar(scores[:], scores[:], row_max[:], None,
                                                ALU.subtract).then_inc(centred, 1)
                        dve.wait_ge(exp_r, t + 1)
                        last = nc.vector.reciprocal(recip[:], row_sum[:])
                        link(last)
                        if layer:
                            link(nc.vector.tensor_scalar(scores[:], scores[:], recip[:], None, ALU.mult))
                            link(nc.vector.tensor_tensor(scores[:], scores[:], mask[:], ALU.mult))
                            link(nc.vector.reduce_max(top[:], scores[:], AX))
                            link(nc.vector.scalar_tensor_tensor(factor[:], top[:], THR, n_valid[:], ALU.is_gt, ALU.mult))
                            link(nc.vector.scalar_tensor_tensor(scores[:], scores[:], THR, scores[:],
                                                                ALU.is_ge, ALU.mult))
                            dve.sem_inc(weights_r, 1)
                        dve.wait_ge(mixed, t + 2)
                        if layer == 0:
                            link(nc.vector.scalar_tensor_tensor(xt, out_ps[:, 0:D], recip[:], xt, ALU.mult, ALU.add))
                        else:
                            link(nc.vector.scalar_tensor_tensor(z[:], out_ps[:, 0:D], factor[:], values[:, t, :],
                                                                ALU.mult, ALU.add))
                            nc.vector.tensor_scalar(zneg[:], z[:], 0.0, None, ALU.min).then_inc(z_r, 1)
                            link(nc.vector.tensor_scalar(z[:], z[:], 0.0, -1.0, ALU.max, ALU.add))
                            dve.wait_ge(e_r, t + 1)
                            link(nc.vector.tensor_tensor(z[:], z[:], zneg[:], ALU.add))
                            link(nc.vector.tensor_tensor(xt, xt, z[:], ALU.add))
                        dve.sem_inc(row_done, 1)
                        link.reset()

                @block.scalar
                def _(act):
                    with act.Fori(0, T) as t:
                        if layer == 0:
                            act.wait_ge(hid_turned, t + 1)
                            nc.scalar.copy(hid_t[:], sm_ps[:, 0:P]).then_inc(hid_kept, 1)
                            act.wait_ge(proj_r, t + 1)
                            nc.scalar.copy(proj_t[:], sm_ps[:, P:2 * P]).then_inc(proj_kept, 1)
                        act.wait_ge(centred, t + 1)
                        nc.scalar.activation(scores[:], scores[:], ACT.Exp, bias=zero_c[:],
                                             scale=1.0 if layer else 1.0 / TEMPERATURE,
                                             accum_out=row_sum[:]).then_inc(exp_r, 1)
                        for c in range(NC):
                            act.wait_ge(turned, t * NC + (c + 1))
                            nc.scalar.copy(p_t[:, c % 2, :], tp_ps[c % 2][:]).then_inc(turned_kept, 1)
                        if layer:
                            act.wait_ge(z_r, t + 1)
                            nc.scalar.activation(zneg[:], zneg[:], ACT.Exp, bias=zero_c[:], scale=1.0).then_inc(e_r, 1)

                @block.tensor
                def _(pe):
                    def mix(c):
                        for q in range(Q):
                            k = c * Q + q
                            last = nc.tensor.matmul(out_ps[:, 0:D], p_t[:, c % 2, q * P:(q + 1) * P], values[:, k, :],
                                                    start=(k == 0), stop=(k == T - 1))
                        return last

                    pe.sem_inc(row_done, 1)
                    with pe.Fori(0, T) as t:
                        if layer == 0:
                            pe.wait_ge(hid_r, t + 1)
                            nc.tensor.transpose(sm_ps[:, 0:P], hid[:], ident[:]).then_inc(hid_turned, 1)
                            pe.wait_ge(hid_kept, t + 1)
                            nc.tensor.matmul(sm_ps[:, P:2 * P], w_sb[:, 0, :], hid_t[:],
                                             start=True, stop=True).then_inc(proj_r, 1)
                            pe.wait_ge(proj_kept, t + 1)
                            for c in range(NC):
                                if c >= 2:
                                    pe.wait_ge(score_used, t * NC + (c - 1))
                                nc.tensor.matmul(sc_ps[c % 2][:], proj_t[:], keys_t[:, c * C:(c + 1) * C],
                                                 start=True, stop=True).then_inc(score_r, 1)
                            pe.wait_ge(exp_r, t + 1)
                        else:
                            pe.wait_ge(weights_r, t + 1)
                        pe.wait_ge(row_done, t + 1)
                        for c in range(NC):
                            if c >= 2:
                                pe.wait_ge(turned_kept, t * NC + (c - 1))
                            for q in range(Q):
                                k = c * Q + q
                                last = nc.tensor.transpose(tp_ps[c % 2][:, q * P:(q + 1) * P],
                                                           scores[:, k * P:(k + 1) * P], ident[:])
                            last.then_inc(turned, 1)
                            if c:
                                pe.wait_ge(turned_kept, t * NC + c)
                                mix(c - 1).then_inc(mixed_part, 1)
                        pe.wait_ge(turned_kept, t * NC + NC)
                        mix(NC - 1).then_inc(mixed, 1)

        mixed_part = sem("mixed_part")
        src_now = sb("src_now", [P, 1])
        attention(0)

        hid_r, hid_turned, hid_kept = sem("hid_r"), sem("hid_turned"), sem("hid_kept")
        both_r, both_kept, parts_r, parts_kept = sem("both_r"), sem("both_kept"), sem("parts_r"), sem("parts_kept")
        valid_kept = sem("valid_kept")
        with nc.Block() as block:
            @block.vector
            def _(dve):
                link = Chain(dve, chain)
                with dve.Fori(0, T) as t:
                    layer_norm_relu(link, x_all[:, t, :]).then_inc(hid_r, 1)
                    dve.wait_ge(parts_r, t + 1)
                    link(nc.vector.tensor_scalar(col_valid[:, bass.ds(t * P, P)], out_ps[:, 0:P], 0.0, None,
                                                 ALU.not_equal))
                    dve.sem_inc(valid_kept, 1)
                    link.reset()

            @block.tensor
            def _(pe):
                pe.wait_ge(bcast_r, 1)
                pe.sem_inc(valid_kept, 1)
                with pe.Fori(0, T) as t:
                    pe.wait_ge(hid_r, t + 1)
                    nc.tensor.transpose(tp_ps[0][:, 0:P], hid[:], ident[:]).then_inc(hid_turned, 1)
                    pe.wait_ge(hid_kept, t + 1)
                    nc.tensor.matmul(tp_ps[1][:, 0:P], hid_t[:], w_sb[:, 1, :], start=True, stop=True)
                    nc.tensor.matmul(tp_ps[1][:, P:2 * P], w_sb[:, 1, :], hid_t[:], start=True,
                                     stop=True).then_inc(both_r, 1)
                    pe.wait_ge(both_kept, 2 * t + 2)
                    pe.wait_ge(valid_kept, t + 1)
                    nc.tensor.matmul(sm_ps[:, 0:P], a_dst_b[:], proj_t[:], start=True, stop=True)
                    nc.tensor.matmul(out_ps[:, 0:P], ones[:], proj_t[:], start=True, stop=True)
                    nc.tensor.matmul(sm_ps[:, 2 * P:2 * P + 1], proj_t[:], a_sb[:, 0:1], start=True,
                                     stop=True).then_inc(parts_r, 1)

            @block.scalar
            def _(act):
                with act.Fori(0, T) as t:
                    act.wait_ge(hid_turned, t + 1)
                    nc.scalar.copy(hid_t[:], tp_ps[0][:, 0:P]).then_inc(hid_kept, 1)
                    act.wait_ge(both_r, t + 1)
                    nc.scalar.copy(values[:, t, :], tp_ps[1][:, 0:P]).then_inc(both_kept, 1)
                    nc.scalar.copy(proj_t[:], tp_ps[1][:, P:2 * P]).then_inc(both_kept, 1)
                    act.wait_ge(parts_r, t + 1)
                    nc.scalar.copy(keys_t[:, bass.ds(t * P, P)], sm_ps[:, 0:P]).then_inc(parts_kept, 1)
                    nc.scalar.copy(src_all[:, bass.ds(t, 1)], sm_ps[:, 2 * P:2 * P + 1]).then_inc(parts_kept, 1)
                    act.wait_ge(parts_kept, 2 * t + 2)

        attention(1)

        stored = sem("stored")
        with nc.Block() as block:
            @block.sync
            def _(sp):
                sp.dma_start(out_v, x_all[:]).then_inc(stored, 16)
                sp.wait_ge(stored, 16)



def fast_path(nc, x, adj, inp, w0, w1, a, out, overflow):
    N, D = x.shape
    T = N // P
    B = 4
    NB = T // B
    FOLD = 512
    BLOCKS = N // FOLD
    HALF = N // 2
    HB = BLOCKS // 2
    RING = 4
    QUARTERS = 4
    NKEY = QUARTERS * 8
    LEVELS = 3
    SLOTS = 16
    G = 3
    EDGES = G * P
    BG = B * G
    LW = SLOTS + 2
    REC = D + 2
    BIAS_E = 127
    FAR = 1e30

    x_v = x.rearrange("(t p) d -> p t d", p=P)
    inp_v = inp.rearrange("(t p) d -> p t d", p=P)
    out_v = out.rearrange("(t p) d -> p t d", p=P)
    a_v = a.rearrange("(k d) o -> d (k o)", k=2)
    table = nc.dram_tensor("table", [N, REC], F32, kind="Internal").ap()
    table_v = table.rearrange("(t p) c -> p t c", p=P)

    ctx = ExitStack()
    with ctx:
        def sb(name, shape, dt=F32):
            return ctx.enter_context(nc.sbuf_tensor(name, shape, dt))

        def sem(name):
            return ctx.enter_context(nc.semaphore(name))

        def bank(name):
            return ctx.enter_context(nc.psum_tensor(name, [P, 512], F32))

        x_all = sb("x_all", [P, T, D])
        h_all = sb("h_all", [P, T, REC])
        inp_sb = h_all[:].rearrange("p t c -> p (t c)")[:, 0:T * D].rearrange("p (t d) -> p t d", d=D)
        src_all = sb("src_all", [P, T])
        ohs_all = sb("ohs_all", [P, NB * BG, SLOTS])
        row_all = sb("row_all", [P, NB * BG])
        idx_all = sb("idx_all", [P, NB * BG], U32)
        se_all = sb("se_all", [P, NB, 2, B])
        ring = sb("ring", [P, RING, HALF], I32)
        sign = sb("sign", [P, 2, HALF], BF16)
        keys = sb("keys", [P, 2, B, QUARTERS, 8], I32)
        cand = sb("cand", [P, B, LEVELS, NKEY])
        lists = sb("lists", [P, 2, B, LW])
        code_i = sb("code_i", [P, B * NKEY], I32)
        code_f = sb("code_f", [P, B * NKEY])
        col_i = sb("col_i", [P, B * NKEY], I32)
        col_f = sb("col_f", [P, B * NKEY])
        exp_i = sb("exp_i", [P, B * NKEY], I32)
        top_i = sb("top_i", [P, B * NKEY], I32)
        valid = sb("valid", [P, 2, B, SLOTS])
        pen = sb("pen", [P, 2, B, SLOTS])
        deg = sb("deg", [P, 2, B])
        empty = sb("empty", [P, 2, B])
        over_rest = sb("over_rest", [P, B * NKEY])
        over_key = sb("over_key", [P, B * QUARTERS])
        over_list = sb("over_list", [P, B])
        over_end = sb("over_end", [P, B])
        over = sb("over", [P, 4])
        over1 = sb("over1", [P, 1])
        ge_start = sb("ge_start", [P, B, EDGES])
        R = sb("R", [P, 2, B, EDGES])
        RT = sb("RT", [P, 2, BG, P])
        led = sb("led", [P, BG, LW])
        pick = sb("pick", [P, BG, SLOTS])
        idx_f = sb("idx_f", [P, BG])
        idx_w = sb("idx_w", [P, 2, BG], U32)
        X = sb("X", [P, 2, BG, REC])
        g_sb = sb("g_sb", [P, B, D])
        hx = sb("hx", [P, B, D])
        hx_t = sb("hx_t", [P, B, P])
        hid = sb("hid", [P, B, D])
        hid_t = sb("hid_t", [P, B, P])
        s_e = sb("s_e", [P, BG])
        prod = sb("prod", [P, BG, D])
        sel = sb("sel", [P, BG, 2, SLOTS])
        sc = sb("sc", [P, B, SLOTS])
        ex = sb("ex", [P, B, SLOTS])
        mx = sb("mx", [P, B])
        sm = sb("sm", [P, B])
        nval = sb("nval", [P, B])
        top = sb("top", [P, B])
        se_w = sb("se_w", [P, 2, B])
        sel_p = sb("sel_p", [P, BG, SLOTS])
        p_e = sb("p_e", [P, BG])
        stats = sb("stats", [P, B, 6])
        mv = sb("mv", [P, 2, B, 2])
        var = sb("var", [P, 2, B])
        rstd = sb("rstd", [P, 2, B])
        shift = sb("shift", [P, 2, B])
        nt1 = sb("nt1", [P, 2, B])
        nt2 = sb("nt2", [P, 2, B])
        z, zn, zr = (prod[:, i * B:(i + 1) * B, :] for i in range(3))
        ident = sb("ident", [P, P])
        ones = sb("ones", [P, P])
        zero_m = sb("zero_m", [P, P])
        tri_lt = sb("tri_lt", [P, P])
        tri_le = sb("tri_le", [P, P])
        bits = sb("bits", [P, BLOCKS, P], BF16)
        key_one = sb("key_one", [P, P], BF16)
        key_add = sb("key_add", [P, FOLD], BF16)
        iota_e = sb("iota_e", [P, EDGES])
        iota_r = sb("iota_r", [P, P])
        slot_of = sb("slot_of", [P, B, G, SLOTS])
        half_c = sb("half_c", [P, 1])
        zero_c = sb("zero_c", [P, 1])
        mean_b = sb("mean_b", [P, D])
        w_sb = sb("w_sb", [P, 2, D])
        w1_t = sb("w1_t", [P, P])
        w1_s = sb("w1_s", [P, 3])
        a_sb = sb("a_sb", [P, 3])

        K = [bank("K0"), bank("K1")]
        SA, SB = bank("SA"), bank("SB")
        GB = [bank("G0"), bank("G1")]
        W0, W1 = bank("W0"), bank("W1")

        adj_loaded = [sem(f"adj_loaded{i}") for i in range(RING)]
        x_loaded, w_loaded, inp_loaded = sem("x_loaded"), sem("w_loaded"), sem("inp_loaded")
        pool_const, pool_chain, chain = sem("pool_const"), sem("pool_chain"), sem("chain")
        wt_r, wt_kept, ws_r, mean_r, init_r = sem("wt_r"), sem("wt_kept"), sem("ws_r"), sem("mean_r"), sem("init_r")
        signed, folded, keys_used = sem("signed"), sem("folded"), sem("keys_used")
        deg_r, pref_r, R_r, lists_r, lists_kept = sem("deg_r"), sem("pref_r"), sem("R_r"), sem("lists_r"), sem("lists_kept")
        idx_r = sem("idx_r")
        X_r = [sem("X_r0"), sem("X_r1")]
        spread_r, spread_used = sem("spread_r"), sem("spread_used")
        so_r, rows_r, centred, ex_r, p_r, pe_r, pe_kept = (sem(s) for s in (
            "so_r", "rows_r", "centred", "ex_r", "p_r", "pe_r", "pe_kept"))
        xs_r, att_r, ln_r = sem("xs_r"), sem("att_r"), sem("ln_r")
        hid_r, hid_turned, hid_kept, h_r, h_kept, rec_r, stored = (sem(s) for s in (
            "hid_r", "hid_turned", "hid_kept", "h_r", "h_kept", "rec_r", "stored"))
        hx_r, hx_turned, hx_kept, g_r, g_kept = (sem(s) for s in ("hx_r", "hx_turned", "hx_kept", "g_r", "g_kept"))
        over_r, over_sum = sem("over_r"), sem("over_sum")

        def tiles(b):
            return bass.ds(b * B, B)

        def edges(b):
            return bass.ds(b * BG, BG)

        def pipeline(eng, step, last):
            for n in range(4):
                step(n, n // 2, n % 2)
            with eng.Fori(2, NB // 2) as k:
                for par in range(2):
                    step(k * 2 + par, k, par, True)
            for n in range(NB, last):
                step(n, n // 2, n % 2)

        def is_in(b, looped):
            return looped or 0 <= b < NB

        def wait(eng, s, value, looped):
            if looped or value > 0:
                eng.wait_ge(s, value)

        def incidence(link, q, ready):
            for t in range(B):
                last = nc.vector.tensor_scalar(ge_start[:, t, :], iota_e[:], se_w[:, 0, t:t + 1], None, ALU.is_ge)
            link(last)
            for t in range(B):
                last = nc.vector.scalar_tensor_tensor(R[:, q, t, :], iota_e[:], se_w[:, 1, t:t + 1], ge_start[:, t, :],
                                                      ALU.is_lt, ALU.mult)
            last.then_inc(ready, 1)

        with nc.Block() as block:
            @block.sync
            def _(sp):
                sp.dma_start(x_all[:], x_v).then_inc(x_loaded, 16)
                sp.dma_start(w_sb[:, 0, :], w0).then_inc(w_loaded, 16)
                sp.dma_start(w_sb[:, 1, :], w1).then_inc(w_loaded, 16)
                sp.dma_start(a_sb[:, 0:2], a_v, allow_slow_non_contiguous=True).then_inc(w_loaded, 16)

                def step(n, k, par, looped=False):
                    if is_in(n - 4, looped):
                        b = n - 4
                        wait(sp, rec_r, b + 1, looped)
                        wait(sp, h_kept, b + 1, looped)
                        sp.dma_start(table_v[:, tiles(b), :], h_all[:, tiles(b), :]).then_inc(stored, 16)
                    if is_in(n, looped):
                        for c in range(2 * B):
                            wait(sp, signed, n * (2 * B) + (c - RING + 1), looped)
                            sp.dma_start(ring[:, c % RING, :],
                                         adj[bass.ds((n * B + c // 2) * P, P), (c % 2) * HALF:(c % 2 + 1) * HALF]
                                         ).then_inc(adj_loaded[c % RING], 16)

                pipeline(sp, step, NB + 4)
                sp.wait_ge(stored, 16 * NB)

            @block.gpsimd
            def _(pool):
                pool.dma_start(inp_sb, inp_v).then_inc(inp_loaded, 16)
                link = Chain(pool, pool_chain)
                pool.memset(ident[:], 0.0)
                pool.memset(bits[:], 0.0)
                pool.memset(key_one[:], 0.0)
                pool.memset(key_add[:], 0.0)
                pool.memset(tri_lt[:], 1.0)
                pool.memset(tri_le[:], 1.0)
                pool.memset(ones[:], 1.0)
                pool.memset(zero_m[:], 0.0)
                pool.memset(half_c[:], -0.5)
                pool.memset(a_sb[:, 2:3], 1.0)
                link(pool.memset(zero_c[:], 0.0))
                for b in range(BLOCKS):
                    last = pool.affine_select(out=bits[:, b, :], in_=bits[:, b, :], compare_op=ALU.not_equal,
                                       fill=float(FOLD // 2 << b), base=0, pattern=[[-1, P]], channel_multiplier=1)
                link(last)
                link(pool.memset(key_one[0:1, :], 1.0))
                link(pool.memset(key_one[32:33, :], 1.0))
                link(pool.memset(key_add[0:1, :], float(FOLD // 2 << BLOCKS)))
                link(pool.iota(key_add[32:33, :], pattern=[[1, FOLD]], base=-(FOLD // 2), channel_multiplier=0,
                               allow_small_or_imprecise_dtypes=True))
                pool.affine_select(out=ident[:], in_=ident[:], compare_op=ALU.not_equal, fill=1.0, base=0,
                                   pattern=[[-1, P]], channel_multiplier=1)
                pool.affine_select(out=tri_lt[:], in_=tri_lt[:], compare_op=ALU.is_gt, fill=0.0, base=0,
                                   pattern=[[1, P]], channel_multiplier=-1)
                pool.affine_select(out=tri_le[:], in_=tri_le[:], compare_op=ALU.is_ge, fill=0.0, base=0,
                                   pattern=[[1, P]], channel_multiplier=-1)
                pool.iota(iota_e[:], pattern=[[1, EDGES]], base=0, channel_multiplier=0,
                          allow_small_or_imprecise_dtypes=True)
                pool.iota(iota_r[:], pattern=[[1, P]], base=1, channel_multiplier=0,
                          allow_small_or_imprecise_dtypes=True)
                pool.iota(slot_of[:], pattern=[[0, B], [P, G], [-1, SLOTS]], base=0, channel_multiplier=1,
                          allow_small_or_imprecise_dtypes=True)
                for q in range(2):
                    last = pool.iota(lists[:, q, :, LW - 1], pattern=[[0, B]], base=1, channel_multiplier=1,
                                     allow_small_or_imprecise_dtypes=True)
                last.then_inc(pool_const, 1)
                link.reset()

                def step(n, k, par, looped=False):
                    if is_in(n - 1, looped):
                        b = n - 1
                        link = Chain(pool, pool_chain)
                        wait(pool, idx_r, b + 1, looped)
                        wait(pool, att_r, b - 1, looped)
                        link.step()
                        for e in range(BG):
                            pool.indirect_dma_start(
                                out=X[:, 1 - par, e, 0:D], out_offset=None, in_=inp,
                                in_offset=bass.IndirectOffsetOnAxis(ap=idx_w[:, 1 - par, e:e + 1], axis=0)
                            ).then_inc(X_r[1 - par], 16)
                        link.reset()

                pipeline(pool, step, NB + 1)

            @block.scalar
            def _(act):
                act.wait_ge(pool_const, 1)
                act.wait_ge(wt_r, 1)
                nc.scalar.copy(w1_t[:], W0[:, 0:P]).then_inc(wt_kept, 1)
                act.wait_ge(ws_r, 1)
                nc.scalar.copy(w1_s[:], W0[:, P:P + 3]).then_inc(wt_kept, 1)
                act.wait_ge(mean_r, 1)
                nc.scalar.mul(mean_b[:], W1[:, 0:D], 1.0 / N).then_inc(wt_kept, 1)

                def step(n, k, par, looped=False):
                    def convert(c):
                        if is_in(n, looped):
                            act.wait_ge(adj_loaded[c % RING], (n * 2 + (c // RING + 1)) * 16)
                            wait(act, folded, n * (2 * B) + (c - 1), looped)
                            nc.scalar.activation(sign[:, c % 2, :], ring[:, c % RING, :], ACT.Sign, bias=half_c[:],
                                                 scale=1.0).then_inc(signed, 1)

                    b1, b2, b3 = n - 1, n - 2, n - 3
                    convert(0)
                    if is_in(b3, looped):
                        wait(act, ln_r, n, looped)
                        wait(act, hid_turned, b3, looped)
                        for t in range(B):
                            last = nc.scalar.activation(hid[:, t, :], x_all[:, b3 * B + t, :], ACT.Relu,
                                                        bias=shift[:, 1, t:t + 1], scale=rstd[:, 1, t:t + 1])
                        last.then_inc(hid_r, 1)
                    convert(1)
                    if is_in(b3, looped):
                        act.wait_ge(hid_turned, b3 + 1)
                        wait(act, h_r, b3, looped)
                        nc.scalar.copy(hid_t[:], W1[:].rearrange("p (b m) -> p b m", b=B)).then_inc(hid_kept, 1)
                    convert(2)
                    if is_in(b3, looped):
                        act.wait_ge(h_r, b3 + 1)
                        nc.scalar.copy(h_all[:, tiles(b3), 0:D], W1[:].rearrange("p (b m) -> p b m", b=B)
                                       ).then_inc(h_kept, 1)
                    convert(3)
                    if is_in(b2, looped):
                        act.wait_ge(centred, b2 + 1)
                        nc.scalar.activation(ex[:], sc[:], ACT.Exp, bias=zero_c[:], scale=1.0 / TEMPERATURE
                                             ).then_inc(ex_r, 1)
                    if is_in(b1, looped):
                        wait(act, ln_r, n, looped)
                        wait(act, hx_turned, b1, looped)
                        for t in range(B):
                            last = nc.scalar.activation(hx[:, t, :], x_all[:, b1 * B + t, :], ACT.Relu,
                                                        bias=shift[:, 0, t:t + 1], scale=rstd[:, 0, t:t + 1])
                        last.then_inc(hx_r, 1)
                    convert(4)
                    convert(5)
                    if is_in(b1, looped):
                        act.wait_ge(hx_turned, b1 + 1)
                        wait(act, g_r, b1, looped)
                        nc.scalar.copy(hx_t[:], W0[:].rearrange("p (b m) -> p b m", b=B)).then_inc(hx_kept, 1)
                    convert(6)
                    convert(7)
                    if is_in(b1, looped):
                        act.wait_ge(g_r, b1 + 1)
                        wait(act, spread_r, B * b1, looped)
                        nc.scalar.copy(g_sb[:], W0[:].rearrange("p (b m) -> p b m", b=B)).then_inc(g_kept, 1)

                pipeline(act, step, NB + 3)

            @block.vector
            def _(dve):
                nc.vector.memset(over_rest[:], 0.0)
                nc.vector.memset(over_key[:], 0.0)
                nc.vector.memset(over_list[:], 0.0)
                nc.vector.memset(over_end[:], 0.0)
                nc.vector.memset(mv[:], 1.0).then_inc(init_r, 1)
                dve.wait_ge(pool_const, 1)
                dve.wait_ge(x_loaded, 16)
                dve.wait_ge(init_r, 1)
                tt, ts, stt = nc.vector.tensor_tensor, nc.vector.tensor_scalar, nc.vector.scalar_tensor_tensor

                def step(n, k, par, looped=False):
                    link = Chain(dve, chain)
                    b1, b2, b3 = n - 1, n - 2, n - 3
                    p1, p2 = 1 - par, par

                    def find(u):
                        if is_in(n, looped):
                            dve.wait_ge(folded, n * (2 * B) + (2 * u + 2))
                            link.step()
                            for q in range(QUARTERS):
                                w = FOLD // QUARTERS
                                last = nc.vector.max(keys[:, par, u, q, :], K[u % 2][:, q * w:(q + 1) * w])
                            last.then_inc(keys_used, 1)

                    def decode():
                        kk = keys[:, p1].rearrange("p b q e -> p (b q e)")
                        ts(code_i[:], kk, 9, None, ALU.logical_shift_right)
                        tt(over_key[:].rearrange("p (b q) -> p b q", q=QUARTERS),
                           over_key[:].rearrange("p (b q) -> p b q", q=QUARTERS), keys[:, p1, :, :, 7], ALU.max)
                        link(ts(col_i[:], kk, FOLD - 1, None, ALU.bitwise_and))
                        nc.vector.tensor_copy(code_f[:], code_i[:])
                        link(ts(col_f[:], col_i[:], float(1 - BIAS_E * FOLD), None, ALU.add))
                        for level in range(LEVELS):
                            ts(exp_i[:], code_f[:].bitcast(I32), 23, None, ALU.logical_shift_right)
                            link(ts(top_i[:], code_f[:].bitcast(I32), 0x7F800000, None, ALU.bitwise_and))
                            stt(cand[:, :, level, :], exp_i[:].rearrange("p (b e) -> p b e", b=B), float(FOLD),
                                col_f[:].rearrange("p (b e) -> p b e", b=B), ALU.mult, ALU.add)
                            link(tt(code_f[:], code_f[:], top_i[:].bitcast(F32), ALU.subtract))
                        tt(over_rest[:], over_rest[:], code_f[:], ALU.max)
                        for t in range(B):
                            last = nc.vector.max(lists[:, p1, t, 0:8], cand[:, t].rearrange("p l e -> p (l e)"))
                        link(last)
                        for t in range(B):
                            last = nc.vector.match_replace(cand[:, t].rearrange("p l e -> p (l e)"),
                                                           lists[:, p1, t, 0:8],
                                                           cand[:, t].rearrange("p l e -> p (l e)"), -FAR)
                        link(last)
                        for t in range(B):
                            last = nc.vector.max(lists[:, p1, t, 8:16], cand[:, t].rearrange("p l e -> p (l e)"))
                        link(last)
                        link(ts(valid[:, p1], lists[:, p1, :, 0:SLOTS], 0.0, None, ALU.is_gt))
                        nc.vector.reduce_sum(deg[:, p1], valid[:, p1], AX).then_inc(deg_r, 1)
                        ts(pen[:, p1], valid[:, p1], -1.0, FAR, ALU.add, ALU.mult)
                        link(tt(over_list[:], over_list[:], lists[:, p1, :, SLOTS - 1], ALU.max))
                        link(ts(empty[:, p1], deg[:, p1], 0.0, None, ALU.is_equal))

                    def record():
                        dve.wait_ge(h_r, b3 + 1)
                        part = SB[:, 448:448 + 3 * B].rearrange("p (b c) -> p b c", c=3)
                        nc.vector.tensor_copy(src_all[:, tiles(b3)], part[:, :, 0])
                        nc.vector.tensor_copy(h_all[:, tiles(b3), D], part[:, :, 1])
                        ts(h_all[:, tiles(b3), D + 1], part[:, :, 2], 0.0, None, ALU.not_equal).then_inc(rec_r, 1)

                    def score():
                        dve.wait_ge(X_r[p2], k * (BG * 16))
                        for t in range(B):
                            dve.wait_ge(spread_r, b2 * B + (t + 1))
                            link.step()
                            for g in range(G):
                                e = t * G + g
                                last = nc.vector.tensor_tensor_reduce(
                                    out=prod[:, e, :], in0=GB[t % 2][:, g * P:(g + 1) * P], in1=X[:, p2, e, 0:D], scale=1.0,
                                    scalar=0.0, op0=ALU.mult, op1=ALU.add, accum_out=s_e[:, e:e + 1])
                            last.then_inc(spread_used, 1)
                        dve.wait_ge(spread_used, b2 * B + B)
                        tt(pick[:], ohs_all[:, edges(b2), :], s_e[:].unsqueeze(2).broadcast_to([P, BG, SLOTS]),
                           ALU.mult).then_inc(so_r, 1)

                    def rows_of_edges():
                        dve.wait_ge(pref_r, b1 + 1)
                        link(nc.vector.tensor_copy(se_all[:, b1], SA[:, 0:2 * B].rearrange("p (s b) -> p s b", s=2)))
                        nc.vector.tensor_copy(se_w[:], se_all[:, b1])
                        nc.vector.tensor_copy(lists[:, p1, :, SLOTS], se_all[:, b1, 0, :])
                        link(tt(over_end[:], over_end[:], se_all[:, b1, 1, :], ALU.max))
                        incidence(link, p1, R_r)

                    def centre():
                        dve.wait_ge(rows_r, b2 + 1)
                        link(tt(sc[:], SB[:, 0:B * SLOTS].rearrange("p (b s) -> p b s", b=B), pen[:, p2], ALU.add))
                        link(nc.vector.reduce_max(mx[:], sc[:], AX))
                        tt(sc[:], sc[:], mx[:].unsqueeze(2).broadcast_to([P, B, SLOTS]), ALU.subtract
                           ).then_inc(centred, 1)

                    def columns_of_edges():
                        dve.wait_ge(lists_r, b1 + 1)
                        nc.vector.tensor_copy(led[:], SA[:, 0:BG * LW].rearrange("p (e c) -> p e c", c=LW)
                                              ).then_inc(lists_kept, 1)
                        dve.wait_ge(lists_kept, b1 + 1)
                        link(tt(ohs_all[:, edges(b1), :], slot_of[:].rearrange("p b g s -> p (b g) s"),
                                led[:, :, SLOTS:SLOTS + 1].broadcast_to([P, BG, SLOTS]), ALU.is_equal))
                        wait(dve, rows_r, b2 + 1, looped)
                        link(tt(pick[:], ohs_all[:, edges(b1), :], led[:, :, 0:SLOTS], ALU.mult))
                        link(nc.vector.reduce_sum(idx_f[:], pick[:], AX))
                        ts(idx_w[:, p1], idx_f[:], 1.0, -1.0, ALU.max, ALU.add).then_inc(idx_r, 1)
                        ts(idx_all[:, edges(b1)], idx_f[:], 1.0, -1.0, ALU.max, ALU.add)
                        link(nc.vector.tensor_copy(row_all[:, edges(b1)], led[:, :, SLOTS + 1]))

                    def normalise():
                        dve.wait_ge(ex_r, b2 + 1)
                        link(tt(ex[:], ex[:], valid[:, p2], ALU.mult))
                        link(nc.vector.reduce_sum(sm[:], ex[:], AX))
                        link(tt(sm[:], sm[:], empty[:, p2], ALU.add))
                        link(nc.vector.reciprocal(sm[:], sm[:]))
                        tt(ex[:], ex[:], sm[:].unsqueeze(2).broadcast_to([P, B, SLOTS]), ALU.mult).then_inc(p_r, 1)

                    def norms():
                        link(ts(var[:], mv[:, :, :, 1], EPS, None, ALU.add))
                        if is_in(b1, looped):
                            dve.wait_ge(hx_r, b1 + 1)
                        if is_in(b3, looped):
                            dve.wait_ge(hid_r, b3 + 1)
                        rsqrt(nc, link, rstd[:], var[:], nt1[:], nt2[:])
                        stt(shift[:], mv[:, :, :, 0], -1.0, rstd[:], ALU.mult, ALU.mult).then_inc(ln_r, 1)

                    find(0)
                    if is_in(b1, looped):
                        dve.wait_ge(keys_used, b1 * B + B)
                        decode()
                    if is_in(b3, looped):
                        record()
                    if is_in(b2, looped):
                        score()
                    find(1)
                    if is_in(b1, looped):
                        rows_of_edges()
                    if is_in(b2, looped):
                        centre()
                    find(2)
                    if is_in(b1, looped):
                        columns_of_edges()
                    if is_in(b2, looped):
                        normalise()
                    if is_in(b1, looped):
                        wait(dve, att_r, b1 - 1, looped)
                        tt(RT[:, p1], iota_r[:].unsqueeze(1).broadcast_to([P, BG, P]),
                           led[:, :, SLOTS + 1:SLOTS + 2].broadcast_to([P, BG, P]), ALU.is_equal)
                    find(3)
                    if is_in(b2, looped):
                        dve.wait_ge(pe_r, b2 + 1)
                        link(tt(sel_p[:], ohs_all[:, edges(b2), :],
                                SB[:, 128:128 + BG * SLOTS].rearrange("p (e s) -> p e s", s=SLOTS), ALU.mult))
                        dve.sem_inc(pe_kept, 1)
                        link(nc.vector.reduce_sum(p_e[:], sel_p[:], AX))
                        tt(X[:, p2, :, 0:D], X[:, p2, :, 0:D], p_e[:].unsqueeze(2).broadcast_to([P, BG, D]), ALU.mult
                           ).then_inc(xs_r, 1)
                    if is_in(n, looped):
                        for t in range(B):
                            last = nc.vector.bn_stats(stats[:, t, :], x_all[:, n * B + t, :])
                        link(last)
                        for t in range(B):
                            last = nc.vector.bn_aggr(mv[:, 0, t, :], stats[:, t, :])
                        link(last)
                    if is_in(b2, looped):
                        dve.wait_ge(att_r, b2 + 1)
                        link(tt(x_all[:, tiles(b2), :], x_all[:, tiles(b2), :],
                                W1[:].rearrange("p (b m) -> p b m", b=B), ALU.add))
                        for t in range(B):
                            last = stt(x_all[:, b2 * B + t, :], mean_b[:], empty[:, p2, t:t + 1],
                                       x_all[:, b2 * B + t, :], ALU.mult, ALU.add)
                        link(last)
                        for t in range(B):
                            last = nc.vector.bn_stats(stats[:, t, :], x_all[:, b2 * B + t, :])
                        link(last)
                        for t in range(B):
                            last = nc.vector.bn_aggr(mv[:, 1, t, :], stats[:, t, :])
                        link(last)
                    if is_in(n, looped) or is_in(b2, looped):
                        norms()
                    link.reset()

                dve.wait_ge(wt_kept, 3)
                pipeline(dve, step, NB + 3)
                link = Chain(dve, chain)
                nc.vector.reduce_max(over[:, 0:1], over_rest[:], AX)
                nc.vector.reduce_max(over[:, 1:2], over_key[:], AX)
                nc.vector.reduce_max(over[:, 2:3], over_list[:], AX)
                link(nc.vector.reduce_max(over[:, 3:4], over_end[:], AX))
                ts(over[:, 0:1], over[:, 0:1], 0.0, None, ALU.is_gt)
                ts(over[:, 1:2], over[:, 1:2], float(FOLD), None, ALU.is_ge)
                ts(over[:, 2:3], over[:, 2:3], 0.0, None, ALU.is_gt)
                link(ts(over[:, 3:4], over[:, 3:4], float(EDGES), None, ALU.is_gt))
                nc.vector.reduce_sum(over1[:], over[:], AX).then_inc(over_r, 1)
                dve.wait_ge(over_sum, 1)
                link(nc.vector.tensor_copy(overflow[0:1, 0:1], SA[0:1, 0:1]))
                link.reset()

            @block.tensor
            def _(pe):
                mm, tr = nc.tensor.matmul, nc.tensor.transpose
                pe.wait_ge(pool_const, 1)
                pe.wait_ge(w_loaded, 48)
                tr(W0[:, 0:P], w_sb[:, 1, :], ident[:]).then_inc(wt_r, 1)
                pe.wait_ge(wt_kept, 1)
                mm(W0[:, P:P + 3], w1_t[:], a_sb[:], start=True, stop=True).then_inc(ws_r, 1)
                pe.wait_ge(inp_loaded, 16)
                mm(W1[:, 0:D], zero_m[:], ident[:], start=True, stop=False)
                with pe.Fori(0, T) as t:
                    mm(W1[:, 0:D], ones[:], inp_sb[:, t, :], start=False, stop=False)
                mm(W1[:, 0:D], zero_m[:], ident[:], start=False, stop=True).then_inc(mean_r, 1)
                pe.wait_ge(wt_kept, 3)

                def step(n, k, par, looped=False):
                    b1, b2, b3 = n - 1, n - 2, n - 3
                    p1, p2 = 1 - par, par

                    def fold(c):
                        if is_in(n, looped):
                            u = c // 2
                            if c % 2 == 0:
                                wait(pe, keys_used, n * B + (u - 1), looped)
                            pe.wait_ge(signed, n * (2 * B) + (c + 1))
                            if c % 2 == 0:
                                mm(K[u % 2][:], key_one[:], key_add[:], start=True, stop=False)
                            for j in range(HB):
                                last = mm(K[u % 2][:], bits[:, (c % 2) * HB + j, :],
                                          sign[:, c % 2, j * FOLD:(j + 1) * FOLD], start=False,
                                          stop=(c % 2 == 1 and j == HB - 1))
                            last.then_inc(folded, 1)

                    def spread(t):
                        if is_in(b2, looped):
                            pe.wait_ge(g_kept, b2 + 1)
                            wait(pe, spread_used, b2 * B + (t - 1), looped)
                            for g in range(G):
                                last = mm(GB[t % 2][:, g * P:(g + 1) * P], R[:, p2, t, g * P:(g + 1) * P],
                                          g_sb[:, t, :], start=True, stop=True)
                            last.then_inc(spread_r, 1)

                    fold(0)
                    fold(1)
                    if is_in(b3, looped):
                        pe.wait_ge(hid_r, b3 + 1)
                        for t in range(B):
                            last = tr(W1[:, t * P:(t + 1) * P], hid[:, t, :], ident[:])
                        last.then_inc(hid_turned, 1)
                    spread(0)
                    spread(1)
                    if is_in(b3, looped):
                        pe.wait_ge(hid_kept, b3 + 1)
                        pe.wait_ge(pe_kept, b3 + 1)
                        for t in range(B):
                            mm(W1[:, t * D:(t + 1) * D], hid_t[:, t, :], w_sb[:, 1, :], start=True, stop=True)
                            last = mm(SB[:, 448 + 3 * t:451 + 3 * t], hid_t[:, t, :], w1_s[:], start=True, stop=True)
                        last.then_inc(h_r, 1)
                    if is_in(b1, looped):
                        pe.wait_ge(deg_r, b1 + 1)
                        wait(pe, lists_kept, b1, looped)
                        mm(SA[:, 0:B], tri_lt[:], deg[:, p1], start=True, stop=True)
                        mm(SA[:, B:2 * B], tri_le[:], deg[:, p1], start=True, stop=True).then_inc(pref_r, 1)
                    spread(2)
                    spread(3)
                    if is_in(b2, looped):
                        pe.wait_ge(so_r, b2 + 1)
                        wait(pe, rec_r, b2, looped)
                        for t in range(B):
                            for g in range(G):
                                last = mm(SB[:, t * SLOTS:(t + 1) * SLOTS], RT[:, p2, t * G + g, :],
                                          pick[:, t * G + g, :], start=(g == 0), stop=(g == G - 1))
                        last.then_inc(rows_r, 1)
                    fold(2)
                    fold(3)
                    if is_in(b1, looped):
                        pe.wait_ge(R_r, b1 + 1)
                        for t in range(B):
                            for g in range(G):
                                e = t * G + g
                                last = mm(SA[:, e * LW:(e + 1) * LW], R[:, p1, t, g * P:(g + 1) * P],
                                          lists[:, p1, t, :], start=True, stop=True)
                        last.then_inc(lists_r, 1)
                    fold(4)
                    if is_in(b1, looped):
                        pe.wait_ge(hx_r, b1 + 1)
                        wait(pe, g_kept, b1, looped)
                        for t in range(B):
                            last = tr(W0[:, t * P:(t + 1) * P], hx[:, t, :], ident[:])
                        last.then_inc(hx_turned, 1)
                    fold(5)
                    if is_in(b2, looped):
                        pe.wait_ge(p_r, b2 + 1)
                        for t in range(B):
                            for g in range(G):
                                e = t * G + g
                                last = mm(SB[:, 128 + e * SLOTS:128 + (e + 1) * SLOTS],
                                          R[:, p2, t, g * P:(g + 1) * P], ex[:, t, :], start=True, stop=True)
                        last.then_inc(pe_r, 1)
                    fold(6)
                    if is_in(b1, looped):
                        pe.wait_ge(hx_kept, b1 + 1)
                        for t in range(B):
                            last = mm(W0[:, t * D:(t + 1) * D], hx_t[:, t, :], w_sb[:, 0, :], start=True, stop=True)
                        last.then_inc(g_r, 1)
                    fold(7)
                    if is_in(b2, looped):
                        pe.wait_ge(xs_r, b2 + 1)
                        wait(pe, h_kept, b2, looped)
                        for t in range(B):
                            for g in range(G):
                                e = t * G + g
                                last = mm(W1[:, t * D:(t + 1) * D], RT[:, p2, e, :], X[:, p2, e, 0:D],
                                          start=(g == 0), stop=(g == G - 1))
                        last.then_inc(att_r, 1)

                pipeline(pe, step, NB + 3)
                pe.wait_ge(over_r, 1)
                mm(SA[0:1, 0:1], over1[:], ones[:, 0:1], start=True, stop=True).then_inc(over_sum, 1)

        idx2_r, take_r, rows2_r, rows2_kept = sem("idx2_r"), sem("take_r"), sem("rows2_r"), sem("rows2_kept")
        X2_r = [sem("X2_r0"), sem("X2_r1")]
        cen2, ex2_r, p2_r, pe2_r, pe2_kept, xs2_r, att2_r = (sem(s) for s in (
            "cen2", "ex2_r", "p2_r", "pe2_r", "pe2_kept", "xs2_r", "att2_r"))
        z_r, e_r, out_r, out_stored, R2_r = sem("z_r"), sem("e_r"), sem("out_r"), sem("out_stored"), sem("R2_r")

        def pipeline1(eng, step, last):
            for n in range(2):
                step(n, n // 2, n % 2)
            with eng.Fori(1, NB // 2) as k:
                for par in range(2):
                    step(k * 2 + par, k, par, True)
            for n in range(NB, last):
                step(n, n // 2, n % 2)

        with nc.Block() as block:
            @block.sync
            def _(sp):
                def step(n, k, par, looped=False):
                    wait(sp, out_r, n + 1, looped)
                    sp.dma_start(out_v[:, tiles(n), :], x_all[:, tiles(n), :]).then_inc(out_stored, 16)

                pipeline1(sp, step, NB)
                sp.wait_ge(out_stored, 16 * NB)

            @block.gpsimd
            def _(pool):
                def step(n, k, par, looped=False):
                    link = Chain(pool, pool_chain)
                    wait(pool, idx2_r, n + 1, looped)
                    wait(pool, att2_r, n - 1, looped)
                    link.step()
                    for e in range(BG):
                        pool.indirect_dma_start(
                            out=X[:, par, e, :], out_offset=None, in_=table,
                            in_offset=bass.IndirectOffsetOnAxis(ap=idx_w[:, par, e:e + 1], axis=0)
                        ).then_inc(X2_r[par], 16)
                    link.reset()

                pipeline1(pool, step, NB)

            @block.scalar
            def _(act):
                def step(n, k, par, looped=False):
                    b1, b2 = n - 1, n - 2
                    if is_in(b1, looped):
                        act.wait_ge(cen2, b1 + 1)
                        nc.scalar.activation(ex[:], sc[:], ACT.Exp, bias=zero_c[:], scale=1.0).then_inc(ex2_r, 1)
                    if is_in(b2, looped):
                        act.wait_ge(z_r, b2 + 1)
                        nc.scalar.activation(zn, zn, ACT.Exp, bias=zero_c[:], scale=1.0)
                        nc.scalar.activation(zr, z, ACT.Relu, bias=zero_c[:], scale=1.0).then_inc(e_r, 1)

                pipeline1(act, step, NB + 2)

            @block.vector
            def _(dve):
                tt, ts, stt = nc.vector.tensor_tensor, nc.vector.tensor_scalar, nc.vector.scalar_tensor_tensor

                def step(n, k, par, looped=False):
                    link = Chain(dve, chain)
                    b1, b2, p1 = n - 1, n - 2, 1 - par
                    if is_in(n, looped):
                        nc.vector.tensor_copy(idx_w[:, par], idx_all[:, edges(n)]).then_inc(idx2_r, 1)
                        wait(dve, R2_r, n, looped)
                        link(nc.vector.tensor_copy(se_w[:], se_all[:, n]))
                    if is_in(b1, looped):
                        dve.wait_ge(X2_r[p1], (k + par) * (BG * 16))
                        for c in range(2):
                            last = tt(sel[:, :, c, :], ohs_all[:, edges(b1), :],
                                      X[:, p1, :, D + c:D + c + 1].broadcast_to([P, BG, SLOTS]), ALU.mult)
                        last.then_inc(take_r, 1)
                    if is_in(n, looped):
                        incidence(link, par, R2_r)
                    if is_in(b1, looped):
                        dve.wait_ge(rows2_r, b1 + 1)
                        both = SA[:, 0:B * 2 * SLOTS].rearrange("p (b c s) -> p b c s", c=2, s=SLOTS)
                        ts(valid[:, 0], both[:, :, 1, :], 0.0, None, ALU.is_gt)
                        link(tt(sc[:], both[:, :, 0, :],
                                src_all[:, tiles(b1)].unsqueeze(2).broadcast_to([P, B, SLOTS]), ALU.add))
                        dve.sem_inc(rows2_kept, 1)
                        ts(pen[:, 0], valid[:, 0], -1.0, FAR, ALU.add, ALU.mult)
                        link(stt(sc[:], sc[:], ALPHA, sc[:], ALU.mult, ALU.max))
                        link(tt(sc[:], sc[:], pen[:, 0], ALU.add))
                        nc.vector.reduce_sum(nval[:], valid[:, 0], AX)
                        link(nc.vector.reduce_max(mx[:], sc[:], AX))
                        tt(sc[:], sc[:], mx[:].unsqueeze(2).broadcast_to([P, B, SLOTS]), ALU.subtract).then_inc(cen2, 1)
                        ts(empty[:, 0], nval[:], 0.0, None, ALU.is_equal)
                    if is_in(n, looped):
                        wait(dve, att2_r, n - 1, looped)
                        tt(RT[:, par], iota_r[:].unsqueeze(1).broadcast_to([P, BG, P]),
                           row_all[:, edges(n)].unsqueeze(2).broadcast_to([P, BG, P]), ALU.is_equal)
                    if is_in(b1, looped):
                        dve.wait_ge(ex2_r, b1 + 1)
                        link(tt(ex[:], ex[:], valid[:, 0], ALU.mult))
                        link(nc.vector.reduce_sum(sm[:], ex[:], AX))
                        link(tt(sm[:], sm[:], empty[:, 0], ALU.add))
                        link(nc.vector.reciprocal(sm[:], sm[:]))
                        link(tt(ex[:], ex[:], sm[:].unsqueeze(2).broadcast_to([P, B, SLOTS]), ALU.mult))
                        link(nc.vector.reduce_max(top[:], ex[:], AX))
                        link(stt(top[:], top[:], THR, nval[:], ALU.is_gt, ALU.mult))
                        link(stt(ex[:], ex[:], THR, ex[:], ALU.is_ge, ALU.mult))
                        tt(ex[:], ex[:], top[:].unsqueeze(2).broadcast_to([P, B, SLOTS]), ALU.mult).then_inc(p2_r, 1)
                    if is_in(b2, looped):
                        dve.wait_ge(att2_r, b2 + 1)
                        link(tt(z, W1[:].rearrange("p (b m) -> p b m", b=B), h_all[:, tiles(b2), 0:D], ALU.add))
                        ts(zn, z, 0.0, None, ALU.min).then_inc(z_r, 1)
                    if is_in(b1, looped):
                        dve.wait_ge(pe2_r, b1 + 1)
                        link(tt(sel_p[:], ohs_all[:, edges(b1), :],
                                SB[:, 0:BG * SLOTS].rearrange("p (e s) -> p e s", s=SLOTS), ALU.mult))
                        dve.sem_inc(pe2_kept, 1)
                        link(nc.vector.reduce_sum(p_e[:], sel_p[:], AX))
                        tt(X[:, p1, :, 0:D], X[:, p1, :, 0:D], p_e[:].unsqueeze(2).broadcast_to([P, BG, D]), ALU.mult
                           ).then_inc(xs2_r, 1)
                    if is_in(b2, looped):
                        dve.wait_ge(e_r, b2 + 1)
                        link(tt(x_all[:, tiles(b2), :], x_all[:, tiles(b2), :], zr, ALU.add))
                        stt(x_all[:, tiles(b2), :], zn, -1.0, x_all[:, tiles(b2), :], ALU.add, ALU.add
                            ).then_inc(out_r, 1)
                    link.reset()

                pipeline1(dve, step, NB + 2)

            @block.tensor
            def _(pe):
                mm = nc.tensor.matmul

                def step(n, k, par, looped=False):
                    b1, p1 = n - 1, 1 - par
                    if is_in(b1, looped):
                        pe.wait_ge(take_r, b1 + 1)
                        wait(pe, rows2_kept, b1, looped)
                        for t in range(B):
                            for g in range(G):
                                e = t * G + g
                                last = mm(SA[:, t * 2 * SLOTS:(t + 1) * 2 * SLOTS], RT[:, p1, e, :],
                                          sel[:, e].rearrange("p c s -> p (c s)"), start=(g == 0), stop=(g == G - 1))
                        last.then_inc(rows2_r, 1)
                        pe.wait_ge(p2_r, b1 + 1)
                        wait(pe, pe2_kept, b1, looped)
                        for t in range(B):
                            for g in range(G):
                                e = t * G + g
                                last = mm(SB[:, e * SLOTS:(e + 1) * SLOTS], R[:, p1, t, g * P:(g + 1) * P],
                                          ex[:, t, :], start=True, stop=True)
                        last.then_inc(pe2_r, 1)
                        pe.wait_ge(xs2_r, b1 + 1)
                        wait(pe, z_r, b1, looped)
                        for t in range(B):
                            for g in range(G):
                                e = t * G + g
                                last = mm(W1[:, t * D:(t + 1) * D], RT[:, p1, e, :], X[:, p1, e, 0:D],
                                          start=(g == 0), stop=(g == G - 1))
                        last.then_inc(att2_r, 1)

                pipeline1(pe, step, NB + 1)


def build(nc, *args):
    with nc.sbuf_tensor("overflow", [P, 1], I32) as overflow:
        fast_path(nc, *args, overflow)
        overflowed = nc.values_load(overflow[0:1, 0:1], min_val=0, max_val=4 * P)
        with nc.If(overflowed > LIMIT):
            dense_path(nc, *args)
        nc.end_ifs()
INPUTS = ["x", "adj", "L0_gnn_input", "L0_gnn_weight", "L1_gnn_W", "L1_gnn_a"]


def kernel(**inputs):
    import numpy as np
    import concourse.bacc as bacc
    from concourse.bass_utils import run_bass_kernel_spmd

    nc = bacc.Bacc("TRN2", target_bir_lowering=False, num_devices=1)
    arrays, args = {}, []
    for name in INPUTS:
        array = np.ascontiguousarray(inputs[name])
        arrays["in_" + name] = array
        args.append(nc.dram_tensor("in_" + name, array.shape, mybir.dt.from_np(array.dtype), kind="ExternalInput").ap())
    out = nc.dram_tensor("out_x", arrays["in_x"].shape, F32, kind="ExternalOutput").ap()
    build(nc, *args, out)
    result = run_bass_kernel_spmd(nc, [arrays], core_ids=[0])
    return result.results[0]["out_x"]
```

```python
import concourse.bass as bass
from concourse import mybir
from contextlib import ExitStack

F32 = mybir.dt.float32
BF16 = mybir.dt.bfloat16
I32 = mybir.dt.int32
U32 = mybir.dt.uint32
U8 = mybir.dt.uint8
ALU = mybir.AluOpType
ACT = mybir.ActivationFunctionType
AX = mybir.AxisListType.X

P = 128
EPS = 1e-5
TEMPERATURE = 0.07
NEG_PAD = float(-2 ** 32 + 1)
NEG = -1000000000.0
THR = 0.0001
ALPHA = 0.2
RSQRT_SEED = float(0x5F3759DF)
LIMIT = 0


class Chain:

    def __init__(self, eng, sem):
        self.eng, self.sem, self.n = eng, sem, 0

    def __call__(self, ins):
        self.n += 1
        ins.then_inc(self.sem, 1)
        self.eng.wait_ge(self.sem, self.n)

    def step(self):
        self.n += 1
        self.eng.sem_inc(self.sem, 1)
        self.eng.wait_ge(self.sem, self.n)

    def reset(self):
        self.eng.sem_clear(self.sem)
        self.n = 0


def rsqrt(nc, link, y, var, tmp, half):
    link(nc.vector.tensor_scalar(half, var, 0.5, None, ALU.mult))
    link(nc.vector.tensor_scalar(y.bitcast(I32), var.bitcast(I32), -0.5, RSQRT_SEED, ALU.mult, ALU.add))
    for _ in range(4):
        link(nc.vector.tensor_tensor(tmp, y, y, ALU.mult))
        link(nc.vector.tensor_tensor(tmp, tmp, half, ALU.mult))
        link(nc.vector.tensor_scalar(tmp, tmp, -1.0, 1.5, ALU.mult, ALU.add))
        link(nc.vector.tensor_tensor(y, y, tmp, ALU.mult))


def dense_path(nc, x, adj, inp, w0, w1, a, out):
    N, D = x.shape
    T = N // P
    C = 512
    NC = N // C
    Q = C // P
    x_v = x.rearrange("(t p) d -> p t d", p=P)
    inp_v = inp.rearrange("(t p) d -> p t d", p=P)
    out_v = out.rearrange("(t p) d -> p t d", p=P)
    a_v = a.rearrange("(k d) o -> d (k o)", k=2)

    with ExitStack() as ctx:
        def sb(name, shape, dt=F32):
            return ctx.enter_context(nc.sbuf_tensor("d_" + name, shape, dt))

        def sem(name):
            return ctx.enter_context(nc.semaphore("d_" + name))

        x_all = sb("x_all", [P, T, D])
        key_in = sb("key_in", [P, D])
        values = sb("values", [P, T, D])
        keys_t = sb("keys_t", [P, N])
        col_valid = sb("col_valid", [P, N], U8)
        adj_sb = sb("adj", [P, N], I32)
        mask = sb("mask", [P, N], U8)
        scores = sb("scores", [P, N])
        w_sb = sb("w", [P, 2, D])
        a_sb = sb("a", [P, 2])
        a_dst_b = sb("a_dst_b", [P, P])
        ones = sb("ones", [P, P])
        ident = sb("ident", [P, P])
        zero_c = sb("zero_c", [P, 1])
        stats = sb("stats", [P, 6])
        mv = sb("mv", [P, 2])
        rstd = sb("rstd", [P, 1])
        nt1 = sb("nt1", [P, 1])
        nt2 = sb("nt2", [P, 1])
        shift = sb("shift", [P, 1])
        hid = sb("hid", [P, D])
        hid_t = sb("hid_t", [P, P])
        proj_t = sb("proj_t", [P, P])
        src_all = sb("src_all", [P, T])
        dst_c = sb("dst_c", [P, P])
        leak = sb("leak", [P, 2, C])
        row_max = sb("row_max", [P, 1])
        row_sum = sb("row_sum", [P, 1])
        recip = sb("recip", [P, 1])
        top = sb("top", [P, 1])
        n_valid = sb("n_valid", [P, 1])
        factor = sb("factor", [P, 1])
        z = sb("z", [P, D])
        zneg = sb("zneg", [P, D])
        p_t = sb("p_t", [P, 2, C])

        def pb(name):
            return ctx.enter_context(nc.psum_tensor("d_" + name, [P, C], F32))
        sc_ps = [pb("sc0"), pb("sc1")]
        tp_ps = [pb("tp0"), pb("tp1")]
        out_ps = pb("out_ps")
        sm_ps = pb("sm_ps")

        loaded, chain = sem("loaded"), sem("chain")
        ident_z, ident_r, ones_r = sem("ident_z"), sem("ident_r"), sem("ones_r")
        bcast_r = sem("bcast_r")

        with nc.Block() as block:
            @block.sync
            def _(sp):
                sp.dma_start(x_all[:], x_v).then_inc(loaded, 16)
                sp.dma_start(values[:], inp_v).then_inc(loaded, 16)
                sp.dma_start(w_sb[:, 0, :], w0).then_inc(loaded, 16)
                sp.dma_start(w_sb[:, 1, :], w1).then_inc(loaded, 16)
                sp.dma_start(a_sb[:], a_v, allow_slow_non_contiguous=True).then_inc(loaded, 16)
                sp.wait_ge(loaded, 80)

            @block.gpsimd
            def _(pool):
                pool.memset(ident[:], 0.0).then_inc(ident_z, 1)
                pool.memset(ones[:], 1.0).then_inc(ones_r, 1)
                pool.memset(zero_c[:], 0.0)
                pool.wait_ge(ident_z, 1)
                pool.affine_select(out=ident[:], in_=ident[:], compare_op=ALU.not_equal, fill=1.0, base=0,
                                   pattern=[[-1, P]], channel_multiplier=1).then_inc(ident_r, 1)

            @block.vector
            def _(dve):
                dve.wait_ge(loaded, 80)
                dve.wait_ge(ones_r, 1)
                nc.vector.tensor_scalar(a_dst_b[:], ones[:], a_sb[:, 1:2], None, ALU.mult).then_inc(bcast_r, 1)

            @block.scalar
            def _(act):
                act.wait_ge(ident_r, 1)

            @block.tensor
            def _(pe):
                pe.wait_ge(ident_r, 1)

        def layer_norm_relu(link, xt):
            link(nc.vector.bn_stats(stats[:], xt))
            link(nc.vector.bn_aggr(mv[:], stats[:]))
            link(nc.vector.tensor_scalar(mv[:, 1:2], mv[:, 1:2], EPS, None, ALU.add))
            rsqrt(nc, link, rstd[:], mv[:, 1:2], nt1[:], nt2[:])
            link(nc.vector.tensor_scalar(hid[:], xt, mv[:, 0:1], rstd[:], ALU.subtract, ALU.mult))
            return nc.vector.tensor_scalar(hid[:], hid[:], 0.0, None, ALU.max)

        with nc.Block() as block:
            key_loaded, key_turned, key_kept = sem("key_loaded"), sem("key_turned"), sem("key_kept")

            @block.sync
            def _(sp):
                sp.sem_inc(key_turned, 1)
                with sp.Fori(0, T) as t:
                    sp.wait_ge(key_turned, t + 1)
                    sp.dma_start(key_in[:], inp_v[:, t, :]).then_inc(key_loaded, 16)

            @block.tensor
            def _(pe):
                pe.wait_ge(ident_r, 1)
                pe.sem_inc(key_kept, 1)
                with pe.Fori(0, T) as t:
                    pe.wait_ge(key_loaded, t * 16 + 16)
                    pe.wait_ge(key_kept, t + 1)
                    nc.tensor.transpose(tp_ps[0][:, 0:P], key_in[:], ident[:]).then_inc(key_turned, 1)

            @block.scalar
            def _(act):
                with act.Fori(0, T) as t:
                    act.wait_ge(key_turned, t + 2)
                    nc.scalar.copy(keys_t[:, bass.ds(t * P, P)], tp_ps[0][:, 0:P]).then_inc(key_kept, 1)

        def attention(layer):
            def lsem(name):
                return sem(f"{name}{layer}")

            adj_loaded, adj_used = lsem("adj_loaded"), lsem("adj_used")
            hid_r, hid_turned, hid_kept = lsem("hid_r"), lsem("hid_turned"), lsem("hid_kept")
            proj_r, proj_kept = lsem("proj_r"), lsem("proj_kept")
            score_r, score_used = lsem("score_r"), lsem("score_used")
            filled, centred, exp_r, weights_r = lsem("filled"), lsem("centred"), lsem("exp_r"), lsem("weights_r")
            turned, turned_kept, mixed = lsem("turned"), lsem("turned_kept"), lsem("mixed")
            pool_step = lsem("pool_step")
            z_r, e_r, row_done = lsem("z_r"), lsem("e_r"), lsem("row_done")

            with nc.Block() as block:
                @block.sync
                def _(sp):
                    sp.sem_inc(adj_used, 1)
                    with sp.Fori(0, T) as t:
                        sp.wait_ge(adj_used, t + 1)
                        sp.dma_start(adj_sb[:], adj[bass.ds(t * P, P), :]).then_inc(adj_loaded, 16)

                @block.gpsimd
                def _(pool):
                    pool.sem_inc(mixed, 1)
                    with pool.Fori(0, T) as t:
                        pool.wait_ge(mixed, t + 1)
                        pool.sem_inc(pool_step, 1)
                        pool.wait_ge(pool_step, 1)
                        pool.memset(scores[:], NEG if layer else NEG_PAD).then_inc(filled, 1)
                        pool.sem_clear(pool_step)

                @block.vector
                def _(dve):
                    link = Chain(dve, chain)
                    with dve.Fori(0, T) as t:
                        xt = x_all[:, t, :]
                        if layer == 0:
                            layer_norm_relu(link, xt).then_inc(hid_r, 1)
                        dve.wait_ge(adj_loaded, t * 16 + 16)
                        if layer == 0:
                            link(nc.vector.tensor_scalar(mask[:], adj_sb[:], 0.0, None, ALU.is_gt))
                        else:
                            link(nc.vector.scalar_tensor_tensor(mask[:], adj_sb[:], 0.0, col_valid[:],
                                                                ALU.is_gt, ALU.mult, accum_out=n_valid[:]))
                        dve.sem_inc(adj_used, 1)
                        dve.wait_ge(filled, t + 1)
                        for c in range(NC):
                            cs = slice(c * C, (c + 1) * C)
                            if layer == 0:
                                dve.wait_ge(score_r, t * NC + (c + 1))
                                link.step()
                                s_new = sc_ps[c % 2][:]
                            else:
                                s_new = leak[:, c % 2, :]
                                link(nc.vector.tensor_scalar(s_new, keys_t[:, cs], src_now[:], None, ALU.add)
                                     if c else nc.vector.tensor_copy(src_now[:], src_all[:, bass.ds(t, 1)]))
                                if c == 0:
                                    link(nc.vector.tensor_scalar(s_new, keys_t[:, cs], src_now[:], None, ALU.add))
                                link(nc.vector.scalar_tensor_tensor(s_new, s_new, ALPHA, s_new, ALU.mult, ALU.max))
                            last = nc.vector.copy_predicated(scores[:, cs], mask[:, cs], s_new)
                            if layer == 0:
                                last.then_inc(score_used, 1)
                        if layer == 0:
                            dve.wait_ge(score_used, t * NC + NC)
                        else:
                            link(last)
                        link(nc.vector.reduce_max(row_max[:], scores[:], AX))
                        nc.vector.tensor_scalar(scores[:], scores[:], row_max[:], None,
                                                ALU.subtract).then_inc(centred, 1)
                        dve.wait_ge(exp_r, t + 1)
                        last = nc.vector.reciprocal(recip[:], row_sum[:])
                        link(last)
                        if layer:
                            link(nc.vector.tensor_scalar(scores[:], scores[:], recip[:], None, ALU.mult))
                            link(nc.vector.tensor_tensor(scores[:], scores[:], mask[:], ALU.mult))
                            link(nc.vector.reduce_max(top[:], scores[:], AX))
                            link(nc.vector.scalar_tensor_tensor(factor[:], top[:], THR, n_valid[:], ALU.is_gt, ALU.mult))
                            link(nc.vector.scalar_tensor_tensor(scores[:], scores[:], THR, scores[:],
                                                                ALU.is_ge, ALU.mult))
                            dve.sem_inc(weights_r, 1)
                        dve.wait_ge(mixed, t + 2)
                        if layer == 0:
                            link(nc.vector.scalar_tensor_tensor(xt, out_ps[:, 0:D], recip[:], xt, ALU.mult, ALU.add))
                        else:
                            link(nc.vector.scalar_tensor_tensor(z[:], out_ps[:, 0:D], factor[:], values[:, t, :],
                                                                ALU.mult, ALU.add))
                            nc.vector.tensor_scalar(zneg[:], z[:], 0.0, None, ALU.min).then_inc(z_r, 1)
                            link(nc.vector.tensor_scalar(z[:], z[:], 0.0, -1.0, ALU.max, ALU.add))
                            dve.wait_ge(e_r, t + 1)
                            link(nc.vector.tensor_tensor(z[:], z[:], zneg[:], ALU.add))
                            link(nc.vector.tensor_tensor(xt, xt, z[:], ALU.add))
                        dve.sem_inc(row_done, 1)
                        link.reset()

                @block.scalar
                def _(act):
                    with act.Fori(0, T) as t:
                        if layer == 0:
                            act.wait_ge(hid_turned, t + 1)
                            nc.scalar.copy(hid_t[:], sm_ps[:, 0:P]).then_inc(hid_kept, 1)
                            act.wait_ge(proj_r, t + 1)
                            nc.scalar.copy(proj_t[:], sm_ps[:, P:2 * P]).then_inc(proj_kept, 1)
                        act.wait_ge(centred, t + 1)
                        nc.scalar.activation(scores[:], scores[:], ACT.Exp, bias=zero_c[:],
                                             scale=1.0 if layer else 1.0 / TEMPERATURE,
                                             accum_out=row_sum[:]).then_inc(exp_r, 1)
                        for c in range(NC):
                            act.wait_ge(turned, t * NC + (c + 1))
                            nc.scalar.copy(p_t[:, c % 2, :], tp_ps[c % 2][:]).then_inc(turned_kept, 1)
                        if layer:
                            act.wait_ge(z_r, t + 1)
                            nc.scalar.activation(zneg[:], zneg[:], ACT.Exp, bias=zero_c[:], scale=1.0).then_inc(e_r, 1)

                @block.tensor
                def _(pe):
                    def mix(c):
                        for q in range(Q):
                            k = c * Q + q
                            last = nc.tensor.matmul(out_ps[:, 0:D], p_t[:, c % 2, q * P:(q + 1) * P], values[:, k, :],
                                                    start=(k == 0), stop=(k == T - 1))
                        return last

                    pe.sem_inc(row_done, 1)
                    with pe.Fori(0, T) as t:
                        if layer == 0:
                            pe.wait_ge(hid_r, t + 1)
                            nc.tensor.transpose(sm_ps[:, 0:P], hid[:], ident[:]).then_inc(hid_turned, 1)
                            pe.wait_ge(hid_kept, t + 1)
                            nc.tensor.matmul(sm_ps[:, P:2 * P], w_sb[:, 0, :], hid_t[:],
                                             start=True, stop=True).then_inc(proj_r, 1)
                            pe.wait_ge(proj_kept, t + 1)
                            for c in range(NC):
                                if c >= 2:
                                    pe.wait_ge(score_used, t * NC + (c - 1))
                                nc.tensor.matmul(sc_ps[c % 2][:], proj_t[:], keys_t[:, c * C:(c + 1) * C],
                                                 start=True, stop=True).then_inc(score_r, 1)
                            pe.wait_ge(exp_r, t + 1)
                        else:
                            pe.wait_ge(weights_r, t + 1)
                        pe.wait_ge(row_done, t + 1)
                        for c in range(NC):
                            if c >= 2:
                                pe.wait_ge(turned_kept, t * NC + (c - 1))
                            for q in range(Q):
                                k = c * Q + q
                                last = nc.tensor.transpose(tp_ps[c % 2][:, q * P:(q + 1) * P],
                                                           scores[:, k * P:(k + 1) * P], ident[:])
                            last.then_inc(turned, 1)
                            if c:
                                pe.wait_ge(turned_kept, t * NC + c)
                                mix(c - 1).then_inc(mixed_part, 1)
                        pe.wait_ge(turned_kept, t * NC + NC)
                        mix(NC - 1).then_inc(mixed, 1)

        mixed_part = sem("mixed_part")
        src_now = sb("src_now", [P, 1])
        attention(0)

        hid_r, hid_turned, hid_kept = sem("hid_r"), sem("hid_turned"), sem("hid_kept")
        both_r, both_kept, parts_r, parts_kept = sem("both_r"), sem("both_kept"), sem("parts_r"), sem("parts_kept")
        valid_kept = sem("valid_kept")
        with nc.Block() as block:
            @block.vector
            def _(dve):
                link = Chain(dve, chain)
                with dve.Fori(0, T) as t:
                    layer_norm_relu(link, x_all[:, t, :]).then_inc(hid_r, 1)
                    dve.wait_ge(parts_r, t + 1)
                    link(nc.vector.tensor_scalar(col_valid[:, bass.ds(t * P, P)], out_ps[:, 0:P], 0.0, None,
                                                 ALU.not_equal))
                    dve.sem_inc(valid_kept, 1)
                    link.reset()

            @block.tensor
            def _(pe):
                pe.wait_ge(bcast_r, 1)
                pe.sem_inc(valid_kept, 1)
                with pe.Fori(0, T) as t:
                    pe.wait_ge(hid_r, t + 1)
                    nc.tensor.transpose(tp_ps[0][:, 0:P], hid[:], ident[:]).then_inc(hid_turned, 1)
                    pe.wait_ge(hid_kept, t + 1)
                    nc.tensor.matmul(tp_ps[1][:, 0:P], hid_t[:], w_sb[:, 1, :], start=True, stop=True)
                    nc.tensor.matmul(tp_ps[1][:, P:2 * P], w_sb[:, 1, :], hid_t[:], start=True,
                                     stop=True).then_inc(both_r, 1)
                    pe.wait_ge(both_kept, 2 * t + 2)
                    pe.wait_ge(valid_kept, t + 1)
                    nc.tensor.matmul(sm_ps[:, 0:P], a_dst_b[:], proj_t[:], start=True, stop=True)
                    nc.tensor.matmul(out_ps[:, 0:P], ones[:], proj_t[:], start=True, stop=True)
                    nc.tensor.matmul(sm_ps[:, 2 * P:2 * P + 1], proj_t[:], a_sb[:, 0:1], start=True,
                                     stop=True).then_inc(parts_r, 1)

            @block.scalar
            def _(act):
                with act.Fori(0, T) as t:
                    act.wait_ge(hid_turned, t + 1)
                    nc.scalar.copy(hid_t[:], tp_ps[0][:, 0:P]).then_inc(hid_kept, 1)
                    act.wait_ge(both_r, t + 1)
                    nc.scalar.copy(values[:, t, :], tp_ps[1][:, 0:P]).then_inc(both_kept, 1)
                    nc.scalar.copy(proj_t[:], tp_ps[1][:, P:2 * P]).then_inc(both_kept, 1)
                    act.wait_ge(parts_r, t + 1)
                    nc.scalar.copy(keys_t[:, bass.ds(t * P, P)], sm_ps[:, 0:P]).then_inc(parts_kept, 1)
                    nc.scalar.copy(src_all[:, bass.ds(t, 1)], sm_ps[:, 2 * P:2 * P + 1]).then_inc(parts_kept, 1)
                    act.wait_ge(parts_kept, 2 * t + 2)

        attention(1)

        stored = sem("stored")
        with nc.Block() as block:
            @block.sync
            def _(sp):
                sp.dma_start(out_v, x_all[:]).then_inc(stored, 16)
                sp.wait_ge(stored, 16)



def fast_path(nc, x, adj, inp, w0, w1, a, out, overflow):
    N, D = x.shape
    T = N // P
    B = 4
    NB = T // B
    FOLD = 512
    BLOCKS = N // FOLD
    HALF = N // 2
    HB = BLOCKS // 2
    RING = 4
    QUARTERS = 4
    NKEY = QUARTERS * 8
    LEVELS = 3
    SLOTS = 16
    G = 3
    EDGES = G * P
    BG = B * G
    LW = SLOTS + 2
    REC = D + 2
    BIAS_E = 127
    FAR = 1e30
    KEY_BITS = 9
    SMALL = 448

    x_v = x.rearrange("(t p) d -> p t d", p=P)
    inp_v = inp.rearrange("(t p) d -> p t d", p=P)
    out_v = out.rearrange("(t p) d -> p t d", p=P)
    a_v = a.rearrange("(k d) o -> d (k o)", k=2)
    table = nc.dram_tensor("table", [N, REC], F32, kind="Internal").ap()
    table_v = table.rearrange("(t p) c -> p t c", p=P)

    ctx = ExitStack()
    with ctx:
        def sb(name, shape, dt=F32):
            return ctx.enter_context(nc.sbuf_tensor(name, shape, dt))

        def sem(name):
            return ctx.enter_context(nc.semaphore(name))

        def bank(name):
            return ctx.enter_context(nc.psum_tensor(name, [P, 512], F32))

        x_all = sb("x_all", [P, T, D])
        h_all = sb("h_all", [P, T, REC])
        inp_sb = h_all[:].rearrange("p t c -> p (t c)")[:, 0:T * D].rearrange("p (t d) -> p t d", d=D)
        src_all = sb("src_all", [P, T])
        ohs_all = sb("ohs_all", [P, NB * BG, SLOTS], BF16)
        row_all = sb("row_all", [P, NB * BG])
        idx_all = sb("idx_all", [P, (NB + 1) * BG], U32)
        se_all = sb("se_all", [P, NB, 2, B])
        ring = sb("ring", [P, RING, HALF], I32)
        sign = sb("sign", [P, RING, HALF], BF16)
        keys = sb("keys", [P, 2, B, QUARTERS, 8], I32)
        cand = sb("cand", [P, B, LEVELS, NKEY])
        lists = sb("lists", [P, 2, B, LW])
        code_f = sb("code_f", [P, B * NKEY])
        col_i = sb("col_i", [P, B * NKEY], I32)
        col_f = sb("col_f", [P, B * NKEY])
        exp_i = sb("exp_i", [P, B * NKEY], I32)
        top_i = sb("top_i", [P, B * NKEY], I32)
        valid = sb("valid", [P, 2, B, SLOTS])
        pen = sb("pen", [P, 2, B, SLOTS])
        deg = sb("deg", [P, 2, B])
        empty_all = sb("empty_all", [P, NB, B])
        over_rest = sb("over_rest", [P, B * NKEY])
        over_key = sb("over_key", [P, B * QUARTERS])
        over_list = sb("over_list", [P, B])
        over_end = sb("over_end", [P, B])
        over = sb("over", [P, 4])
        over1 = sb("over1", [P, 1])
        R = sb("R", [P, 2, B, EDGES])
        RT = sb("RT", [P, 2, BG, P])
        led = sb("led", [P, BG, LW])
        pick = sb("pick", [P, BG, SLOTS])
        idx_f = sb("idx_f", [P, BG])
        idx_w = sb("idx_w", [P, 4, BG], U32)
        X = sb("X", [P, 2, BG, REC])
        g_sb = sb("g_sb", [P, B, D])
        mean_of_empty = sb("mean_of_empty", [P, B, D])
        hx = sb("hx", [P, B, D])
        hx_t = sb("hx_t", [P, B, P])
        hid = sb("hid", [P, B, D])
        hid_t = sb("hid_t", [P, B, P])
        s_e = sb("s_e", [P, BG])
        prod = sb("prod", [P, BG, D])
        sel = sb("sel", [P, BG, 2, SLOTS])
        sc = sb("sc", [P, B, SLOTS])
        ex = sb("ex", [P, B, SLOTS])
        mx = sb("mx", [P, B])
        sm = sb("sm", [P, B])
        nval = sb("nval", [P, B])
        top = sb("top", [P, B])
        se_w = sb("se_w", [P, 2, B])
        sel_p = sb("sel_p", [P, BG, SLOTS])
        p_e = sb("p_e", [P, BG])
        stats = sb("stats", [P, B, 6])
        mv = sb("mv", [P, 2, B, 2])
        var = sb("var", [P, 2, B])
        rstd = sb("rstd", [P, 2, B])
        shift = sb("shift", [P, 2, B])
        half_var = sb("half_var", [P, 2, B])
        newton = sb("newton", [P, 2, B])
        ge_start = prod[:].rearrange("p e d -> p (e d)").rearrange("p (t e) -> p t e", t=B)
        ring_f = ring[:].rearrange("p r c -> p (r c)").bitcast(F32)
        z, zn, zr = (ring_f[:, i * B * D:(i + 1) * B * D].rearrange("p (b d) -> p b d", d=D) for i in range(3))
        ident = sb("ident", [P, P])
        ones = sb("ones", [P, P])
        inp_sum = sb("inp_sum", [P, D])
        tri_lt = sb("tri_lt", [P, P])
        tri_le = sb("tri_le", [P, P])
        bits = sb("bits", [P, BLOCKS, P], BF16)
        key_one = sb("key_one", [P, P], BF16)
        key_add = sb("key_add", [P, FOLD], BF16)
        iota_e = sb("iota_e", [P, EDGES])
        iota_r = sb("iota_r", [P, P])
        slot_of = sb("slot_of", [P, B, G, SLOTS])
        half_c = sb("half_c", [P, 1])
        zero_c = sb("zero_c", [P, 1])
        mean_b = sb("mean_b", [P, D])
        w_sb = sb("w_sb", [P, 2, D])
        w1_t = sb("w1_t", [P, P])
        w1_s = sb("w1_s", [P, 3])
        a_sb = sb("a_sb", [P, 3])

        K = [bank("K0"), bank("K1")]
        SA, SB = bank("SA"), bank("SB")
        G0, G1 = bank("G0"), bank("G1")
        W0, W1 = bank("W0"), bank("W1")
        GB = [G0, G1, W0, G0]

        adj_loaded = [sem(f"adj_loaded{i}") for i in range(RING)]
        x_loaded, w_loaded, inp_loaded = sem("x_loaded"), sem("w_loaded"), sem("inp_loaded")
        key_const, pool_const, pool_chain, chain = sem("key_const"), sem("pool_const"), sem("pool_chain"), sem("chain")
        wt_r, wt_kept, ws_r, mean_r, init_r = sem("wt_r"), sem("wt_kept"), sem("ws_r"), sem("mean_r"), sem("init_r")
        ws_kept, mean_kept, inp_summed, empty_r, mean_added, RT_r, pe_sum_r = (sem(s) for s in (
            "ws_kept", "mean_kept", "inp_summed", "empty_r", "mean_added", "RT_r", "pe_sum_r"))
        signed, folded, keys_used = sem("signed"), sem("folded"), sem("keys_used")
        deg_r, pref_r, R_r, lists_r, lists_kept = sem("deg_r"), sem("pref_r"), sem("R_r"), sem("lists_r"), sem("lists_kept")
        idx_r = sem("idx_r")
        X_r = [sem("X_r0"), sem("X_r1")]
        spread_r, spread_used = sem("spread_r"), sem("spread_used")
        so_r, rows_r, centred, ex_r, p_r, pe_r, pe_kept = (sem(s) for s in (
            "so_r", "rows_r", "centred", "ex_r", "p_r", "pe_r", "pe_kept"))
        xs_r, att_r, ln_r = sem("xs_r"), sem("att_r"), sem("ln_r")
        hid_r, hid_turned, hid_kept, h_r, h_kept, rec_r, stored = (sem(s) for s in (
            "hid_r", "hid_turned", "hid_kept", "h_r", "h_kept", "rec_r", "stored"))
        hx_r, hx_turned, hx_kept, g_r, g_kept = (sem(s) for s in ("hx_r", "hx_turned", "hx_kept", "g_r", "g_kept"))
        over_r, over_sum = sem("over_r"), sem("over_sum")

        def tiles(b):
            return bass.ds(b * B, B)

        def edges(b):
            return bass.ds(b * BG, BG)

        def pipeline(eng, step, last):
            for n in range(4):
                step(n, n // 2, n % 2)
            with eng.Fori(2, NB // 2) as k:
                for par in range(2):
                    step(k * 2 + par, k, par, True)
            for n in range(NB, last):
                step(n, n // 2, n % 2)

        def is_in(b, looped):
            return looped or 0 <= b < NB

        def wait(eng, s, value, looped):
            if looped or value > 0:
                eng.wait_ge(s, value)

        def incidence(link, q, ready):
            for t in range(B):
                last = nc.vector.tensor_scalar(ge_start[:, t, :], iota_e[:], se_w[:, 0, t:t + 1], None, ALU.is_ge)
            link(last)
            for t in range(B):
                last = nc.vector.scalar_tensor_tensor(R[:, q, t, :], iota_e[:], se_w[:, 1, t:t + 1], ge_start[:, t, :],
                                                      ALU.is_lt, ALU.mult)
            last.then_inc(ready, 1)

        scratch = [3 * B * D]

        def part(width):
            start = scratch[0]
            scratch[0] += width
            assert scratch[0] <= RING * HALF
            return ring_f[:, start:start + width]

        X4 = [X[:, q] for q in range(2)] + [part(BG * REC).rearrange("p (e c) -> p e c", c=REC) for _ in range(2)]
        RT4 = [RT[:, q] for q in range(2)] + [part(BG * P).rearrange("p (e r) -> p e r", r=P) for _ in range(2)]
        R4 = ([R[:, q].rearrange("p b e -> p (b e)") for q in range(2)] + [part(BG * P) for _ in range(2)])
        ex2 = [ex, part(B * SLOTS).rearrange("p (b s) -> p b s", s=SLOTS)]
        def late(b):
            return isinstance(b, int) and b == NB - 1

        def x_of(b, q):
            return X4[2] if late(b) else X[:, q]

        def att_of(b):
            return {NB - 2: K[1], NB - 1: K[0]}.get(b, W1) if isinstance(b, int) else W1

        def rt_of(b, q):
            return RT4[2] if late(b) else RT[:, q]

        with nc.Block() as block:
            @block.sync
            def _(sp):
                def step(n, k, par, looped=False):
                    if is_in(n, looped):
                        for c in range(2 * B):
                            wait(sp, signed, n * (2 * B) + (c - RING + 1), looped)
                            sp.dma_start(ring[:, c % RING, :],
                                         adj[bass.ds((n * B + c // 2) * P, P), (c % 2) * HALF:(c % 2 + 1) * HALF]
                                         ).then_inc(adj_loaded[c % RING], 16)
                            if not looped and n == 0 and c == RING - 1:
                                sp.dma_start(x_all[:], x_v).then_inc(x_loaded, 16)
                                sp.dma_start(w_sb[:, 0, :], w0).then_inc(w_loaded, 16)
                                sp.dma_start(w_sb[:, 1, :], w1).then_inc(w_loaded, 16)
                                sp.dma_start(a_sb[:, 0:2], a_v, allow_slow_non_contiguous=True).then_inc(w_loaded, 16)
                            if not looped and n == 0 and c == 2 * B - 1:
                                sp.dma_start(inp_sb, inp_v).then_inc(inp_loaded, 16)
                    if is_in(n - 4, looped):
                        b = n - 4
                        wait(sp, rec_r, b + 1, looped)
                        wait(sp, h_kept, b + 1, looped)
                        sp.dma_start(table_v[:, tiles(b), :], h_all[:, tiles(b), :]).then_inc(stored, 16)

                pipeline(sp, step, NB + 4)
                sp.wait_ge(stored, 16 * NB)

            @block.gpsimd
            def _(pool):
                link = Chain(pool, pool_chain)
                pool.memset(half_c[:], -0.5)
                pool.memset(bits[:], 0.0)
                pool.memset(key_one[:], 0.0)
                link(pool.memset(key_add[:], 0.0))
                for b in range(BLOCKS):
                    last = pool.affine_select(out=bits[:, b, :], in_=bits[:, b, :], compare_op=ALU.not_equal,
                                       fill=float(FOLD // 2 << b), base=0, pattern=[[-1, P]], channel_multiplier=1)
                link(last)
                link(pool.memset(key_one[0:1, :], 1.0))
                link(pool.memset(key_one[32:33, :], 1.0))
                link(pool.memset(key_add[0:1, :], float(FOLD // 2 << BLOCKS)))
                pool.iota(key_add[32:33, :], pattern=[[1, FOLD]], base=-(FOLD // 2), channel_multiplier=0,
                          allow_small_or_imprecise_dtypes=True).then_inc(key_const, 1)
                pool.wait_ge(key_const, 1)
                pool.memset(ident[:], 0.0)
                pool.memset(tri_lt[:], 1.0)
                pool.memset(tri_le[:], 1.0)
                pool.memset(ones[:], 1.0)
                pool.memset(a_sb[:, 2:3], 1.0)
                link(pool.memset(zero_c[:], 0.0))
                pool.affine_select(out=ident[:], in_=ident[:], compare_op=ALU.not_equal, fill=1.0, base=0,
                                   pattern=[[-1, P]], channel_multiplier=1)
                pool.affine_select(out=tri_lt[:], in_=tri_lt[:], compare_op=ALU.is_gt, fill=0.0, base=0,
                                   pattern=[[1, P]], channel_multiplier=-1)
                pool.affine_select(out=tri_le[:], in_=tri_le[:], compare_op=ALU.is_ge, fill=0.0, base=0,
                                   pattern=[[1, P]], channel_multiplier=-1)
                pool.iota(iota_e[:], pattern=[[1, EDGES]], base=0, channel_multiplier=0,
                          allow_small_or_imprecise_dtypes=True)
                pool.iota(iota_r[:], pattern=[[1, P]], base=1, channel_multiplier=0,
                          allow_small_or_imprecise_dtypes=True)
                pool.iota(slot_of[:], pattern=[[0, B], [P, G], [-1, SLOTS]], base=0, channel_multiplier=1,
                          allow_small_or_imprecise_dtypes=True)
                for q in range(2):
                    last = pool.iota(lists[:, q, :, LW - 1], pattern=[[0, B]], base=1, channel_multiplier=1,
                                     allow_small_or_imprecise_dtypes=True)
                last.then_inc(pool_const, 1)
                pool.wait_ge(pool_const, 1)
                link.reset()

                def step(n, k, par, looped=False):
                    b1, b2, b3, p1 = n - 1, n - 2, n - 3, 1 - par
                    link = Chain(pool, pool_chain)
                    if is_in(b3, looped) and (looped or n < NB):
                        pool.wait_ge(pe_sum_r, b3 + 1)
                        pool.tensor_tensor(X[:, p1, :, 0:D], X[:, p1, :, 0:D],
                                           p_e[:].unsqueeze(2).broadcast_to([P, BG, D]), ALU.mult).then_inc(xs_r, 1)
                    if is_in(b1, looped):
                        wait(pool, idx_r, b1 + 1, looped)
                        if not late(b1):
                            wait(pool, att_r, b1 - 1, looped)
                        link.step()
                        for e in range(BG):
                            pool.indirect_dma_start(
                                out=x_of(b1, p1)[:, e, 0:D], out_offset=None, in_=inp,
                                in_offset=bass.IndirectOffsetOnAxis(ap=idx_w[:, p1, e:e + 1], axis=0)
                            ).then_inc(X_r[p1], 16)
                    if is_in(b2, looped):
                        if not looped and n == 2:
                            pool.wait_ge(mean_kept, 1)
                        pool.wait_ge(hx_r, b2 + 1)
                        pool.wait_ge(empty_r, b2 + 1)
                        link.step()
                        link(pool.tensor_tensor(mean_of_empty[:], mean_b[:].unsqueeze(1).broadcast_to([P, B, D]),
                                                empty_all[:, b2].unsqueeze(2).broadcast_to([P, B, D]), ALU.mult))
                        pool.tensor_tensor(x_all[:, tiles(b2), :], x_all[:, tiles(b2), :], mean_of_empty[:], ALU.add
                                           ).then_inc(mean_added, 1)
                        pool.wait_ge(mean_added, b2 + 1)
                    link.step()
                    link.reset()

                pipeline(pool, step, NB + 3)

            @block.scalar
            def _(act):
                act.wait_ge(key_const, 1)

                def step(n, k, par, looped=False):
                    b1, b2, b3, b4 = n - 1, n - 2, n - 3, n - 4

                    def convert(c):
                        if is_in(n, looped):
                            act.wait_ge(adj_loaded[c % RING], (n * 2 + (c // RING + 1)) * 16)
                            wait(act, folded, n * (2 * B) + (c - RING + 1), looped)
                            nc.scalar.activation(sign[:, c % RING, :], ring[:, c % RING, :], ACT.Sign, bias=half_c[:],
                                                 scale=1.0).then_inc(signed, 1)

                    def hidden_x():
                        if is_in(b1, looped):
                            wait(act, ln_r, n, looped)
                            wait(act, hx_turned, b1, looped)
                            for t in range(B):
                                last = nc.scalar.activation(hx[:, t, :], x_all[:, b1 * B + t, :], ACT.Relu,
                                                            bias=shift[:, 0, t:t + 1], scale=rstd[:, 0, t:t + 1])
                            last.then_inc(hx_r, 1)

                    def keep_turned_x():
                        if is_in(b1, looped):
                            act.wait_ge(hx_turned, b1 + 1)
                            wait(act, g_r, b1, looped)
                            nc.scalar.copy(hx_t[:], W0[:].rearrange("p (b m) -> p b m", b=B)).then_inc(hx_kept, 1)

                    def keep_g():
                        if is_in(b2, looped):
                            act.wait_ge(g_r, b2 + 1)
                            wait(act, spread_r, B * b2, looped)
                            nc.scalar.copy(g_sb[:], W0[:].rearrange("p (b m) -> p b m", b=B)).then_inc(g_kept, 1)

                    def keep_h(b):
                        if is_in(b, looped):
                            act.wait_ge(h_r, b + 1)
                            nc.scalar.copy(h_all[:, tiles(b), 0:D], W1[:].rearrange("p (b m) -> p b m", b=B)
                                           ).then_inc(h_kept, 1)

                    def exponent():
                        if is_in(b2, looped):
                            act.wait_ge(centred, b2 + 1)
                            nc.scalar.activation(ex[:], sc[:], ACT.Exp, bias=zero_c[:], scale=1.0 / TEMPERATURE
                                                 ).then_inc(ex_r, 1)

                    def hidden(b):
                        if is_in(b, looped):
                            wait(act, ln_r, n, looped)
                            wait(act, hid_turned, b, looped)
                            for t in range(B):
                                last = nc.scalar.activation(hid[:, t, :], x_all[:, b * B + t, :], ACT.Relu,
                                                            bias=shift[:, 1, t:t + 1], scale=rstd[:, 1, t:t + 1])
                            last.then_inc(hid_r, 1)

                    def keep_turned(b):
                        if is_in(b, looped):
                            act.wait_ge(hid_turned, b + 1)
                            wait(act, h_r, b, looped)
                            nc.scalar.copy(hid_t[:], W1[:].rearrange("p (b m) -> p b m", b=B)).then_inc(hid_kept, 1)

                    if not looped and n >= NB:
                        keep_g()
                        if n == NB:
                            keep_h(b4)
                            hidden_x()
                            exponent()
                            keep_turned_x()
                        else:
                            hidden(b4)
                            exponent()
                            keep_turned(b4)
                            keep_h(b4)
                        return
                    convert(0)
                    convert(1)
                    keep_g()
                    keep_h(b4)
                    if not looped and n == 1:
                        act.wait_ge(wt_r, 1)
                        nc.scalar.copy(w1_t[:], W0[:, 0:P]).then_inc(wt_kept, 1)
                        act.wait_ge(ws_r, 1)
                        nc.scalar.copy(w1_s[:], W0[:, P:P + 3]).then_inc(ws_kept, 1)
                    if not looped and n == 2:
                        act.wait_ge(mean_r, 1)
                        nc.scalar.mul(mean_b[:], W1[:, 0:D], 1.0 / N).then_inc(mean_kept, 1)
                    convert(2)
                    convert(3)
                    convert(4)
                    convert(5)
                    exponent()
                    convert(6)
                    hidden_x()
                    hidden(b3)
                    convert(7)
                    keep_turned_x()
                    keep_turned(b3)

                pipeline(act, step, NB + 4)

            @block.vector
            def _(dve):
                nc.vector.memset(over_rest[:], 0.0)
                nc.vector.memset(over_key[:], 0.0)
                nc.vector.memset(over_list[:], 0.0)
                nc.vector.memset(over_end[:], 0.0)
                nc.vector.memset(idx_all[:, NB * BG:(NB + 1) * BG], 0)
                nc.vector.memset(mv[:], 1.0).then_inc(init_r, 1)
                dve.wait_ge(init_r, 1)
                tt, ts, stt = nc.vector.tensor_tensor, nc.vector.tensor_scalar, nc.vector.scalar_tensor_tensor

                def step(n, k, par, looped=False):
                    link = Chain(dve, chain)
                    b1, b2, b3, b4 = n - 1, n - 2, n - 3, n - 4
                    p1, p2 = 1 - par, par

                    def find(b, q_b, u):
                        if is_in(b, looped):
                            dve.wait_ge(folded, b * (2 * B) + (2 * u + 2))
                            link.step()
                            for q in range(QUARTERS):
                                w = FOLD // QUARTERS
                                last = nc.vector.max(keys[:, q_b, u, q, :], K[u % 2][:, q * w:(q + 1) * w])
                            last.then_inc(keys_used, 1)

                    def decode():
                        kk = keys[:, p1].rearrange("p b q e -> p (b q e)")
                        nc.vector.tensor_copy(code_f[:], kk)
                        tt(over_key[:].rearrange("p (b q) -> p b q", q=QUARTERS),
                           over_key[:].rearrange("p (b q) -> p b q", q=QUARTERS), keys[:, p1, :, :, 7], ALU.max)
                        link(ts(col_i[:], kk, FOLD - 1, None, ALU.bitwise_and))
                        link(ts(col_f[:], col_i[:], float(1 - (BIAS_E + KEY_BITS) * FOLD), None, ALU.add))
                        for level in range(LEVELS):
                            ts(exp_i[:], code_f[:].bitcast(I32), 23, None, ALU.logical_shift_right)
                            link(ts(top_i[:], code_f[:].bitcast(I32), 0x7F800000, None, ALU.bitwise_and))
                            stt(cand[:, :, level, :], exp_i[:].rearrange("p (b e) -> p b e", b=B), float(FOLD),
                                col_f[:].rearrange("p (b e) -> p b e", b=B), ALU.mult, ALU.add)
                            link(tt(code_f[:], code_f[:], top_i[:].bitcast(F32), ALU.subtract))
                        tt(over_rest[:], over_rest[:], code_f[:], ALU.max)
                        for t in range(B):
                            last = nc.vector.max(lists[:, p1, t, 0:8], cand[:, t].rearrange("p l e -> p (l e)"))
                        link(last)
                        for t in range(B):
                            last = nc.vector.match_replace(cand[:, t].rearrange("p l e -> p (l e)"),
                                                           lists[:, p1, t, 0:8],
                                                           cand[:, t].rearrange("p l e -> p (l e)"), -FAR)
                        link(last)
                        for t in range(B):
                            last = nc.vector.max(lists[:, p1, t, 8:16], cand[:, t].rearrange("p l e -> p (l e)"))
                        link(last)
                        link(ts(valid[:, p1], lists[:, p1, :, 0:SLOTS], 0.0, None, ALU.is_gt))
                        nc.vector.reduce_sum(deg[:, p1], valid[:, p1], AX).then_inc(deg_r, 1)
                        ts(pen[:, p1], valid[:, p1], -1.0, FAR, ALU.add, ALU.mult)
                        link(tt(over_list[:], over_list[:], lists[:, p1, :, SLOTS - 1], ALU.max))
                        ts(empty_all[:, b1], deg[:, p1], 0.0, None, ALU.is_equal).then_inc(empty_r, 1)

                    def record(b):
                        dve.wait_ge(h_r, b + 1)
                        part = SA[:, SMALL:SMALL + 3 * B].rearrange("p (b c) -> p b c", c=3)
                        nc.vector.tensor_copy(src_all[:, tiles(b)], part[:, :, 0])
                        nc.vector.tensor_copy(h_all[:, tiles(b), D], part[:, :, 1])
                        ts(h_all[:, tiles(b), D + 1], part[:, :, 2], 0.0, None, ALU.not_equal).then_inc(rec_r, 1)

                    def score():
                        dve.wait_ge(X_r[p2], k * (BG * 16))
                        for t in range(B):
                            dve.wait_ge(spread_r, b2 * B + (t + 1))
                            link.step()
                            for g in range(G):
                                e = t * G + g
                                last = nc.vector.tensor_tensor_reduce(
                                    out=prod[:, e, :], in0=GB[t][:, g * P:(g + 1) * P], in1=x_of(b2, p2)[:, e, 0:D], scale=1.0,
                                    scalar=0.0, op0=ALU.mult, op1=ALU.add, accum_out=s_e[:, e:e + 1])
                            last.then_inc(spread_used, 1)
                        dve.wait_ge(spread_used, b2 * B + B)
                        tt(pick[:], ohs_all[:, edges(b2), :], s_e[:].unsqueeze(2).broadcast_to([P, BG, SLOTS]),
                           ALU.mult).then_inc(so_r, 1)

                    def rows_of_edges():
                        dve.wait_ge(pref_r, b1 + 1)
                        link(nc.vector.tensor_copy(se_all[:, b1], SA[:, 0:2 * B].rearrange("p (s b) -> p s b", s=2)))
                        nc.vector.tensor_copy(se_w[:], se_all[:, b1])
                        nc.vector.tensor_copy(lists[:, p1, :, SLOTS], se_all[:, b1, 0, :])
                        link(tt(over_end[:], over_end[:], se_all[:, b1, 1, :], ALU.max))
                        incidence(link, p1, R_r)

                    def centre():
                        dve.wait_ge(rows_r, b2 + 1)
                        link(tt(sc[:], SB[:, 0:B * SLOTS].rearrange("p (b s) -> p b s", b=B), pen[:, p2], ALU.add))
                        link(nc.vector.reduce_max(mx[:], sc[:], AX))
                        tt(sc[:], sc[:], mx[:].unsqueeze(2).broadcast_to([P, B, SLOTS]), ALU.subtract
                           ).then_inc(centred, 1)

                    def columns_of_edges():
                        dve.wait_ge(lists_r, b1 + 1)
                        nc.vector.tensor_copy(led[:], SA[:, 0:BG * LW].rearrange("p (e c) -> p e c", c=LW)
                                              ).then_inc(lists_kept, 1)
                        dve.wait_ge(lists_kept, b1 + 1)
                        link(tt(ohs_all[:, edges(b1), :], slot_of[:].rearrange("p b g s -> p (b g) s"),
                                led[:, :, SLOTS:SLOTS + 1].broadcast_to([P, BG, SLOTS]), ALU.is_equal))
                        wait(dve, rows_r, b2 if late(b1) else b2 + 1, looped)
                        link(tt(pick[:], ohs_all[:, edges(b1), :], led[:, :, 0:SLOTS], ALU.mult))
                        link(nc.vector.reduce_sum(idx_f[:], pick[:], AX))
                        ts(idx_w[:, p1], idx_f[:], 1.0, -1.0, ALU.max, ALU.add).then_inc(idx_r, 1)
                        tt(rt_of(b1, p1), iota_r[:].unsqueeze(1).broadcast_to([P, BG, P]),
                           led[:, :, SLOTS + 1:SLOTS + 2].broadcast_to([P, BG, P]), ALU.is_equal).then_inc(RT_r, 1)
                        ts(idx_all[:, edges(b1)], idx_f[:], 1.0, -1.0, ALU.max, ALU.add)
                        link(nc.vector.tensor_copy(row_all[:, edges(b1)], led[:, :, SLOTS + 1]))

                    def normalise():
                        dve.wait_ge(ex_r, b2 + 1)
                        link(tt(ex[:], ex[:], valid[:, p2], ALU.mult))
                        link(nc.vector.reduce_sum(sm[:], ex[:], AX))
                        link(tt(sm[:], sm[:], empty_all[:, b2], ALU.add))
                        link(nc.vector.reciprocal(sm[:], sm[:]))
                        tt(ex[:], ex[:], sm[:].unsqueeze(2).broadcast_to([P, B, SLOTS]), ALU.mult).then_inc(p_r, 1)

                    def shares():
                        dve.wait_ge(pe_r, b3 + 1)
                        link(tt(sel_p[:], ohs_all[:, edges(b3), :],
                                SB[:, 128:128 + BG * SLOTS].rearrange("p (e s) -> p e s", s=SLOTS), ALU.mult))
                        last = nc.vector.reduce_sum(p_e[:], sel_p[:], AX)
                        if looped or n < NB:
                            last.then_inc(pe_sum_r, 1)
                        else:
                            link(last)

                    def share_neighbours():
                        nbr = x_of(b3, p1)[:, :, 0:D]
                        tt(nbr, nbr, p_e[:].unsqueeze(2).broadcast_to([P, BG, D]), ALU.mult).then_inc(xs_r, 1)

                    def moments(which, b):
                        for t in range(B):
                            last = nc.vector.bn_stats(stats[:, t, :], x_all[:, b * B + t, :])
                        link(last)
                        for t in range(B):
                            last = nc.vector.bn_aggr(mv[:, which, t, :], stats[:, t, :])
                        link(last)

                    def add_attention():
                        dve.wait_ge(mean_added, b3 + 1)
                        dve.wait_ge(att_r, b3 + 1)
                        link(tt(x_all[:, tiles(b3), :], x_all[:, tiles(b3), :],
                                att_of(b3)[:].rearrange("p (b m) -> p b m", b=B), ALU.add))
                        moments(1, b3)

                    def norms(first=False):
                        ts(var[:], mv[:, :, :, 1], EPS, None, ALU.add)
                        link(ts(half_var[:], mv[:, :, :, 1], EPS, -0.5, ALU.add, ALU.mult))
                        if looped or 0 <= b2:
                            dve.wait_ge(hx_r, b2 + 1 if looped or n < NB or first else NB)
                        if is_in(b4, looped):
                            dve.wait_ge(hid_r, b4 + 1)
                        link(ts(rstd[:].bitcast(I32), var[:].bitcast(I32), -0.5, RSQRT_SEED, ALU.mult, ALU.add))
                        for _ in range(3):
                            link(tt(newton[:], rstd[:], rstd[:], ALU.mult))
                            link(tt(newton[:], newton[:], half_var[:], ALU.mult))
                            link(stt(rstd[:], newton[:], 1.5, rstd[:], ALU.add, ALU.mult))
                        stt(shift[:], mv[:, :, :, 0], -1.0, rstd[:], ALU.mult, ALU.mult).then_inc(ln_r, 1)

                    if not looped and n == 1:
                        dve.wait_ge(pool_const, 1)
                    if not looped and n >= NB:
                        if n == NB:
                            find(b1, p1, 3)
                            dve.wait_ge(keys_used, b1 * B + B)
                            decode()
                            record(b4)
                            norms(first=True)
                            rows_of_edges()
                            columns_of_edges()
                        if is_in(b3, looped):
                            shares()
                        if is_in(b2, looped):
                            score()
                        if is_in(b3, looped):
                            share_neighbours()
                        if n == NB + 2:
                            record(b4 - 1)
                        if is_in(b2, looped):
                            centre()
                            normalise()
                        if is_in(b3, looped):
                            add_attention()
                            norms()
                        if n > NB + 1:
                            record(b4)
                        link.step()
                        link.reset()
                        return
                    find(b1, p1, 3)
                    if is_in(b1, looped):
                        dve.wait_ge(keys_used, b1 * B + B)
                        decode()
                    if is_in(b4, looped):
                        record(b4)
                    if is_in(b3, looped):
                        shares()
                    if is_in(b2, looped):
                        score()
                    find(n, par, 0)
                    if is_in(b1, looped):
                        rows_of_edges()
                    if is_in(b2, looped):
                        centre()
                    if is_in(b3, looped):
                        add_attention()
                    if is_in(b1, looped) or is_in(b3, looped):
                        norms()
                    find(n, par, 1)
                    if is_in(b1, looped):
                        columns_of_edges()
                    if is_in(b2, looped):
                        normalise()
                    find(n, par, 2)
                    if is_in(n, looped):
                        if not looped and n == 0:
                            dve.wait_ge(x_loaded, 16)
                        moments(0, n)
                    if not looped and n == 0:
                        dve.wait_ge(inp_loaded, 16)
                        nc.vector.reduce_sum(inp_sum[:], inp_sb.rearrange("p t d -> p d t"), AX).then_inc(inp_summed, 1)
                    link.step()
                    link.reset()

                pipeline(dve, step, NB + 4)

            @block.tensor
            def _(pe):
                mm, tr = nc.tensor.matmul, nc.tensor.transpose
                pe.wait_ge(key_const, 1)

                def step(n, k, par, looped=False):
                    b1, b2, b3, b4 = n - 1, n - 2, n - 3, n - 4
                    p1, p2 = 1 - par, par

                    def fold(c):
                        if is_in(n, looped):
                            u = c // 2
                            if c % 2 == 0:
                                wait(pe, keys_used, n * B + (u - 1), looped)
                            pe.wait_ge(signed, n * (2 * B) + (c + 1))
                            if c % 2 == 0:
                                mm(K[u % 2][:], key_one[:], key_add[:], start=True, stop=False)
                            for j in range(HB):
                                last = mm(K[u % 2][:], bits[:, (c % 2) * HB + j, :],
                                          sign[:, c % RING, j * FOLD:(j + 1) * FOLD], start=False,
                                          stop=(c % 2 == 1 and j == HB - 1))
                            last.then_inc(folded, 1)

                    def spread(t):
                        if is_in(b2, looped):
                            pe.wait_ge(g_kept, b2 + 1)
                            if t == B - 1:
                                pe.wait_ge(spread_used, b2 * B + 1)
                            else:
                                wait(pe, spread_used, b2 * B, looped)
                            for g in range(G):
                                last = mm(GB[t][:, g * P:(g + 1) * P], R[:, p2, t, g * P:(g + 1) * P],
                                          g_sb[:, t, :], start=True, stop=True)
                            last.then_inc(spread_r, 1)

                    def first_edges():
                        if is_in(b1, looped):
                            pe.wait_ge(deg_r, b1 + 1)
                            wait(pe, lists_kept, b1, looped)
                            wait(pe, rec_r, b3, looped)
                            mm(SA[:, 0:B], tri_lt[:], deg[:, p1], start=True, stop=True)
                            mm(SA[:, B:2 * B], tri_le[:], deg[:, p1], start=True, stop=True).then_inc(pref_r, 1)

                    def rows():
                        if is_in(b2, looped):
                            pe.wait_ge(so_r, b2 + 1)
                            pe.wait_ge(RT_r, b2 + 1)
                            for t in range(B):
                                for g in range(G):
                                    last = mm(SB[:, t * SLOTS:(t + 1) * SLOTS], rt_of(b2, p2)[:, t * G + g, :],
                                              pick[:, t * G + g, :], start=(g == 0), stop=(g == G - 1))
                            last.then_inc(rows_r, 1)

                    def attend():
                        if is_in(b3, looped):
                            pe.wait_ge(xs_r, b3 + 1)
                            if att_of(b3) is W1:
                                wait(pe, h_kept, b3, looped)
                            for t in range(B):
                                for g in range(G):
                                    e = t * G + g
                                    last = mm(att_of(b3)[:, t * D:(t + 1) * D], rt_of(b3, p1)[:, e, :], x_of(b3, p1)[:, e, 0:D],
                                              start=(g == 0), stop=(g == G - 1))
                            last.then_inc(att_r, 1)

                    def edges_lists():
                        if is_in(b1, looped):
                            pe.wait_ge(R_r, b1 + 1)
                            for t in range(B):
                                for g in range(G):
                                    e = t * G + g
                                    last = mm(SA[:, e * LW:(e + 1) * LW], R[:, p1, t, g * P:(g + 1) * P],
                                              lists[:, p1, t, :], start=True, stop=True)
                            last.then_inc(lists_r, 1)

                    def turn_hx():
                        if is_in(b1, looped):
                            pe.wait_ge(hx_r, b1 + 1)
                            wait(pe, g_kept, b1, looped)
                            for t in range(B):
                                last = tr(W0[:, t * P:(t + 1) * P], hx[:, t, :], ident[:])
                            last.then_inc(hx_turned, 1)

                    def turn_hid(b):
                        if is_in(b, looped):
                            pe.wait_ge(hid_r, b + 1)
                            if not looped and n > NB:
                                pe.wait_ge(h_kept, b)
                            for t in range(B):
                                last = tr(W1[:, t * P:(t + 1) * P], hid[:, t, :], ident[:])
                            last.then_inc(hid_turned, 1)

                    def edge_shares():
                        if is_in(b2, looped):
                            pe.wait_ge(p_r, b2 + 1)
                            for t in range(B):
                                for g in range(G):
                                    e = t * G + g
                                    last = mm(SB[:, 128 + e * SLOTS:128 + (e + 1) * SLOTS],
                                              R[:, p2, t, g * P:(g + 1) * P], ex[:, t, :], start=True, stop=True)
                            last.then_inc(pe_r, 1)

                    def project_hx():
                        if is_in(b1, looped):
                            pe.wait_ge(hx_kept, b1 + 1)
                            for t in range(B):
                                last = mm(W0[:, t * D:(t + 1) * D], hx_t[:, t, :], w_sb[:, 0, :], start=True, stop=True)
                            last.then_inc(g_r, 1)

                    def project_hid(b):
                        if is_in(b, looped):
                            pe.wait_ge(hid_kept, b + 1)
                            wait(pe, lists_kept, b1 + 1 if looped else min(b1 + 1, NB), looped)
                            if not looped and n > NB:
                                pe.wait_ge(rec_r, b)
                            for t in range(B):
                                mm(W1[:, t * D:(t + 1) * D], hid_t[:, t, :], w_sb[:, 1, :], start=True, stop=True)
                                last = mm(SA[:, SMALL + 3 * t:SMALL + 3 * t + 3], hid_t[:, t, :], w1_s[:],
                                          start=True, stop=True)
                            last.then_inc(h_r, 1)

                    if not looped and n >= NB:
                        first_edges()
                        for t in range(B - 1):
                            spread(t)
                        edges_lists()
                        spread(B - 1)
                        rows()
                        turn_hx()
                        attend()
                        if n > NB:
                            turn_hid(b4)
                        edge_shares()
                        project_hx()
                        if n > NB:
                            project_hid(b4)
                        return
                    for t in range(B - 1):
                        spread(t)
                    fold(0)
                    first_edges()
                    spread(B - 1)
                    fold(1)
                    if not looped and n == 1:
                        pe.wait_ge(pool_const, 1)
                        pe.wait_ge(w_loaded, 48)
                        tr(W0[:, 0:P], w_sb[:, 1, :], ident[:]).then_inc(wt_r, 1)
                        pe.wait_ge(wt_kept, 1)
                        mm(W0[:, P:P + 3], w1_t[:], a_sb[:], start=True, stop=True).then_inc(ws_r, 1)
                    if not looped and n == 2:
                        pe.wait_ge(inp_summed, 1)
                        mm(W1[:, 0:D], ones[:], inp_sum[:], start=True, stop=True).then_inc(mean_r, 1)
                    rows()
                    attend()
                    fold(2)
                    fold(3)
                    edges_lists()
                    fold(4)
                    fold(5)
                    turn_hx()
                    turn_hid(b3)
                    fold(6)
                    fold(7)
                    edge_shares()
                    project_hx()
                    project_hid(b3)

                pipeline(pe, step, NB + 4)

        DEEP = 4
        idx2_r, take_r, rows2_r, RT2_r, turned, R2_r = (sem(s) for s in (
            "idx2_r", "take_r", "rows2_r", "RT2_r", "turned", "R2_r"))
        X2_r = [sem(f"X2_r{i}") for i in range(DEEP)]
        cen2, ex2_r, p2_r, pe2_r, pe2_sum_r, xs2_r, att2_r = (sem(s) for s in (
            "cen2", "ex2_r", "p2_r", "pe2_r", "pe2_sum_r", "xs2_r", "att2_r"))

        def att2_of(b):
            return {NB - 3: W0, NB - 2: G1, NB - 1: K[0]}.get(b, W1) if isinstance(b, int) else W1

        z_r, e_r, out_r, out_stored = sem("z_r"), sem("e_r"), sem("out_r"), sem("out_stored")

        turn = [K[0], K[1], G0]

        def pipeline1(eng, step, last):
            for n in range(DEEP):
                step(n, 0, n)
            with eng.Fori(1, NB // DEEP) as k:
                for q in range(DEEP):
                    step(k * DEEP + q, k, q, True)
            for n in range(NB, last):
                step(n, n // DEEP, n % DEEP)

        with nc.Block() as block:
            @block.sync
            def _(sp):
                def step(n, k, q, looped=False):
                    if is_in(n - 3, looped):
                        b3 = n - 3
                        wait(sp, out_r, b3 + 1, looped)
                        sp.dma_start(out_v[:, tiles(b3), :], x_all[:, tiles(b3), :]).then_inc(out_stored, 16)

                pipeline1(sp, step, NB + 3)
                sp.wait_ge(out_stored, 16 * NB)

            @block.gpsimd
            def _(pool):
                def step(n, k, q, looped=False):
                    link = Chain(pool, pool_chain)
                    wait(pool, idx2_r, n + 1, looped)
                    wait(pool, att2_r, n - (DEEP - 1), looped)
                    link.step()
                    for e in range(BG):
                        pool.indirect_dma_start(
                            out=X4[q][:, e, :], out_offset=None, in_=table,
                            in_offset=bass.IndirectOffsetOnAxis(ap=idx_w[:, q, e:e + 1], axis=0)
                        ).then_inc(X2_r[q], 16)
                    link.reset()

                pipeline1(pool, step, NB)

            @block.scalar
            def _(act):
                def step(n, k, q, looped=False):
                    b1, b2, b4 = n - 1, n - 2, n - 4
                    q2 = (q - 2) % DEEP
                    def elu_parts(b):
                        if is_in(b, looped):
                            act.wait_ge(z_r, b + 1)
                            nc.scalar.activation(zn, zn, ACT.Exp, bias=zero_c[:], scale=1.0)
                            nc.scalar.activation(zr, z, ACT.Relu, bias=zero_c[:], scale=1.0).then_inc(e_r, 1)

                    def exponent():
                        if is_in(b1, looped):
                            act.wait_ge(cen2, b1 + 1)
                            nc.scalar.activation(ex2[(q - 1) % 2][:], sc[:], ACT.Exp, bias=zero_c[:], scale=1.0
                                                 ).then_inc(ex2_r, 1)

                    if not looped and n >= NB:
                        exponent()
                        if n == NB + 1:
                            elu_parts(b4 - 1)
                        if n > NB:
                            elu_parts(b4)
                        return
                    elu_parts(b4)
                    exponent()
                    if is_in(b2, looped):
                        act.wait_ge(pe2_sum_r, b2 + 1)
                        for e in range(BG):
                            last = nc.scalar.activation(X4[q2][:, e, 0:D], X4[q2][:, e, 0:D], ACT.Identity,
                                                        bias=zero_c[:], scale=p_e[:, e:e + 1])
                        last.then_inc(xs2_r, 1)
                    if is_in(n, looped):
                        wait(act, turned, n + 1, looped)
                        wait(act, pe2_r, n - (DEEP - 1), looped)
                        for i in range(G):
                            last = nc.scalar.copy(R4[q][:, i * 512:(i + 1) * 512], turn[i][:])
                        last.then_inc(R2_r, 1)

                pipeline1(act, step, NB + 4)

            @block.vector
            def _(dve):
                tt, ts, stt = nc.vector.tensor_tensor, nc.vector.tensor_scalar, nc.vector.scalar_tensor_tensor

                def step(n, k, q, looped=False):
                    link = Chain(dve, chain)
                    b1, b2, b4 = n - 1, n - 2, n - 4
                    q1, q2 = (q - 1) % DEEP, (q - 2) % DEEP
                    if is_in(n + 1, looped):
                        nc.vector.tensor_copy(idx_w[:, (q + 1) % DEEP], idx_all[:, edges(n + 1)]).then_inc(idx2_r, 1)
                    def take():
                        if is_in(b1, looped):
                            dve.wait_ge(X2_r[q1], (k + (1 if q else 0)) * (BG * 16))
                            for c in range(2):
                                last = tt(sel[:, :, c, :], ohs_all[:, edges(b1), :],
                                          X4[q1][:, :, D + c:D + c + 1].broadcast_to([P, BG, SLOTS]), ALU.mult)
                            last.then_inc(take_r, 1)

                    def sum_up(b):
                        if is_in(b, looped):
                            dve.wait_ge(att2_r, b + 1)
                            link(tt(z, att2_of(b)[:].rearrange("p (b m) -> p b m", b=B), h_all[:, tiles(b), 0:D], ALU.add))
                            ts(zn, z, 0.0, None, ALU.min).then_inc(z_r, 1)

                    def normalise():
                        if is_in(b2, looped):
                            dve.wait_ge(ex2_r, b2 + 1)
                            p = ex2[q2 % 2]
                            known = valid[:, q2 % 2]
                            nc.vector.reduce_sum(nval[:], known, AX)
                            link(tt(p[:], p[:], known, ALU.mult))
                            link(nc.vector.reduce_sum(sm[:], p[:], AX))
                            link(stt(sm[:], nval[:], 0.0, sm[:], ALU.is_equal, ALU.add))
                            nc.vector.reduce_max(top[:], p[:], AX)
                            link(nc.vector.reciprocal(sm[:], sm[:]))
                            tt(top[:], top[:], sm[:], ALU.mult)
                            link(tt(p[:], p[:], sm[:].unsqueeze(2).broadcast_to([P, B, SLOTS]), ALU.mult))
                            link(stt(top[:], top[:], THR, nval[:], ALU.is_gt, ALU.mult))
                            link(stt(p[:], p[:], THR, p[:], ALU.is_ge, ALU.mult))
                            tt(p[:], p[:], top[:].unsqueeze(2).broadcast_to([P, B, SLOTS]), ALU.mult).then_inc(p2_r, 1)

                    def edge_rows():
                        if is_in(n, looped):
                            tt(RT4[q], iota_r[:].unsqueeze(1).broadcast_to([P, BG, P]),
                               row_all[:, edges(n)].unsqueeze(2).broadcast_to([P, BG, P]), ALU.is_equal).then_inc(RT2_r, 1)

                    def centre():
                        if is_in(b1, looped):
                            dve.wait_ge(rows2_r, b1 + 1)
                            both = SA[:, 0:B * 2 * SLOTS].rearrange("p (b c s) -> p b c s", c=2, s=SLOTS)
                            ts(valid[:, q1 % 2], both[:, :, 1, :], 0.0, None, ALU.is_gt)
                            link(tt(sc[:], both[:, :, 0, :],
                                    src_all[:, tiles(b1)].unsqueeze(2).broadcast_to([P, B, SLOTS]), ALU.add))
                            ts(pen[:, 0], valid[:, q1 % 2], -1.0, FAR, ALU.add, ALU.mult)
                            link(stt(sc[:], sc[:], ALPHA, sc[:], ALU.mult, ALU.max))
                            link(tt(sc[:], sc[:], pen[:, 0], ALU.add))
                            link(nc.vector.reduce_max(mx[:], sc[:], AX))
                            tt(sc[:], sc[:], mx[:].unsqueeze(2).broadcast_to([P, B, SLOTS]), ALU.subtract).then_inc(cen2, 1)

                    def result(b):
                        if is_in(b, looped):
                            dve.wait_ge(e_r, b + 1)
                            link(tt(x_all[:, tiles(b), :], x_all[:, tiles(b), :], zr, ALU.add))
                            stt(x_all[:, tiles(b), :], zn, -1.0, x_all[:, tiles(b), :], ALU.add, ALU.add
                                ).then_inc(out_r, 1)

                    def shares():
                        if is_in(b2, looped):
                            dve.wait_ge(pe2_r, b2 + 1)
                            wait(dve, xs2_r, b2, looped)
                            link(tt(sel_p[:], ohs_all[:, edges(b2), :],
                                    SB[:, 0:BG * SLOTS].rearrange("p (e s) -> p e s", s=SLOTS), ALU.mult))
                            nc.vector.reduce_sum(p_e[:], sel_p[:], AX).then_inc(pe2_sum_r, 1)
                            if not looped and n >= NB:
                                dve.wait_ge(pe2_sum_r, b2 + 1)
                                tt(X4[q2][:, :, 0:D], X4[q2][:, :, 0:D],
                                   p_e[:].unsqueeze(2).broadcast_to([P, BG, D]), ALU.mult).then_inc(xs2_r, 1)

                    if not looped and n >= NB:
                        take()
                        normalise()
                        centre()
                        if n == NB + 1:
                            sum_up(b4 - 1)
                            result(b4 - 1)
                        shares()
                        if n > NB:
                            sum_up(b4)
                            result(b4)
                    else:
                        take()
                        sum_up(b4)
                        normalise()
                        edge_rows()
                        centre()
                        result(b4)
                        shares()
                    link.step()
                    link.reset()

                nc.vector.tensor_copy(idx_w[:, 0], idx_all[:, edges(0)]).then_inc(idx2_r, 1)
                link = Chain(dve, chain)
                nc.vector.reduce_max(over[:, 0:1], over_rest[:], AX)
                nc.vector.reduce_max(over[:, 1:2], over_key[:], AX)
                nc.vector.reduce_max(over[:, 2:3], over_list[:], AX)
                link(nc.vector.reduce_max(over[:, 3:4], over_end[:], AX))
                ts(over[:, 0:1], over[:, 0:1], float(FOLD), None, ALU.is_ge)
                ts(over[:, 1:2], over[:, 1:2], float(FOLD), None, ALU.is_ge)
                ts(over[:, 2:3], over[:, 2:3], 0.0, None, ALU.is_gt)
                link(ts(over[:, 3:4], over[:, 3:4], float(EDGES), None, ALU.is_gt))
                nc.vector.reduce_sum(over1[:], over[:], AX).then_inc(over_r, 1)
                dve.wait_ge(over_sum, 1)
                link(nc.vector.tensor_copy(overflow[0:1, 0:1], SA[0:1, 0:1]))
                link.reset()
                pipeline1(dve, step, NB + 4)

            @block.tensor
            def _(pe):
                mm, tr = nc.tensor.matmul, nc.tensor.transpose

                def step(n, k, q, looped=False):
                    b1, b2, b3 = n - 1, n - 2, n - 3
                    q1, q2, q3 = ((q - i) % DEEP for i in (1, 2, 3))
                    if is_in(b1, looped):
                        pe.wait_ge(take_r, b1 + 1)
                        wait(pe, cen2, b1, looped)
                        for t in range(B):
                            for g in range(G):
                                e = t * G + g
                                last = mm(SA[:, t * 2 * SLOTS:(t + 1) * 2 * SLOTS], RT4[q1][:, e, :],
                                          sel[:, e].rearrange("p c s -> p (c s)"), start=(g == 0), stop=(g == G - 1))
                        last.then_inc(rows2_r, 1)

                    def attend():
                        if is_in(b3, looped):
                            pe.wait_ge(xs2_r, b3 + 1)
                            if att2_of(b3) is W1:
                                wait(pe, z_r, b3, looped)
                            for t in range(B):
                                for g in range(G):
                                    e = t * G + g
                                    last = mm(att2_of(b3)[:, t * D:(t + 1) * D], RT4[q3][:, e, :], X4[q3][:, e, 0:D],
                                              start=(g == 0), stop=(g == G - 1))
                            last.then_inc(att2_r, 1)

                    def edge_shares():
                        if is_in(b2, looped):
                            pe.wait_ge(p2_r, b2 + 1)
                            pe.wait_ge(R2_r, b2 + 1)
                            wait(pe, pe2_sum_r, b2, looped)
                            for t in range(B):
                                for g in range(G):
                                    e = t * G + g
                                    last = mm(SB[:, e * SLOTS:(e + 1) * SLOTS], R4[q2][:, e * P:(e + 1) * P],
                                              ex2[q2 % 2][:, t, :], start=True, stop=True)
                            last.then_inc(pe2_r, 1)

                    if not looped and n >= NB:
                        edge_shares()
                        attend()
                    else:
                        attend()
                        edge_shares()
                    if is_in(n, looped):
                        wait(pe, RT2_r, n + 1, looped)
                        wait(pe, R2_r, n, looped)
                        for e in range(BG):
                            last = tr(turn[e // 4][:, e % 4 * P:(e % 4 + 1) * P], RT4[q][:, e, :], ident[:])
                        last.then_inc(turned, 1)

                pe.wait_ge(over_r, 1)
                mm(SA[0:1, 0:1], over1[:], ones[:, 0:1], start=True, stop=True).then_inc(over_sum, 1)
                pipeline1(pe, step, NB + 3)


def build(nc, *args):
    with nc.sbuf_tensor("overflow", [P, 1], I32) as overflow:
        fast_path(nc, *args, overflow)
        overflowed = nc.values_load(overflow[0:1, 0:1], min_val=0, max_val=4 * P)
        with nc.If(overflowed > LIMIT):
            dense_path(nc, *args)
        nc.end_ifs()
INPUTS = ["x", "adj", "L0_gnn_input", "L0_gnn_weight", "L1_gnn_W", "L1_gnn_a"]


def kernel(**inputs):
    import numpy as np
    import concourse.bacc as bacc
    from concourse.bass_utils import run_bass_kernel_spmd

    nc = bacc.Bacc("TRN2", target_bir_lowering=False, num_devices=1)
    arrays, args = {}, []
    for name in INPUTS:
        array = np.ascontiguousarray(inputs[name])
        arrays["in_" + name] = array
        args.append(nc.dram_tensor("in_" + name, array.shape, mybir.dt.from_np(array.dtype), kind="ExternalInput").ap())
    out = nc.dram_tensor("out_x", arrays["in_x"].shape, F32, kind="ExternalOutput").ap()
    build(nc, *args, out)
    result = run_bass_kernel_spmd(nc, [arrays], core_ids=[0])
    return result.results[0]["out_x"]
```
